# Optimizing a Trainium2 kernel written in Bass

```python
import numpy as np
import jax
import jax.numpy as jnp

def _softmax(x, axis=-1):
    return jax.nn.softmax(x, axis=axis)

def _gelu(x):
    return jax.nn.gelu(x, approximate=True)

def _silu(x):
    return jax.nn.silu(x)

def _sigmoid(x):
    return jax.nn.sigmoid(x)

def _layernorm(x, axis=-1, eps=1e-05):
    m = jnp.mean(x, axis=axis, keepdims=True)
    v = jnp.var(x, axis=axis, keepdims=True)
    return (x - m) / jnp.sqrt(v + eps)

def _scatter_add(tgt, idx, src, axis=0):
    return tgt.at[idx].add(src)

def _segment_sum(src, seg, n):
    return jax.ops.segment_sum(src, seg, n)
kernel_name = 'mk_flamingo_gated_d1_seqx_r8_5860fe'

def setup_inputs(seed: int=0):
    np.random.seed(seed)
    _w = jnp.asarray

    def _rec_inputs():
        import jax
        import jax.numpy as jnp
        _rk = jax.random.key(seed)
        x = -0.0005146 + 1 * jax.random.normal(jax.random.fold_in(_rk, 1), (64, 64, 128), jnp.float32)
        _lenS = 64 - jax.random.randint(jax.random.fold_in(_rk, 7), (64,), 0, max(1, 64 // 4) + 1, jnp.int32)
        _lenS2 = 64 - jax.random.randint(jax.random.fold_in(_rk, 8), (64,), 0, max(1, 64 // 4) + 1, jnp.int32)
        _ctx_1024P = jax.random.normal(jax.random.fold_in(_rk, 11), (64, 16, 128), jnp.float32)
        _ctx_1024c = jax.random.dirichlet(jax.random.fold_in(_rk, 511), 0.3 * jnp.ones((16,), jnp.float32), (64, 64))
        _ctx_1024t = jnp.einsum('bsk,bkd->bsd', _ctx_1024c, _ctx_1024P)
        _ctx_1024t = _ctx_1024t * jax.lax.rsqrt(jnp.mean(jnp.square(_ctx_1024t)) + 1e-12) * 0.953939
        ctx_1024 = -0.000292821 + 1.00034 * (_ctx_1024t + 0.3 * jax.random.normal(jax.random.fold_in(_rk, 611), (64, 64, 128), jnp.float32))
        _g = jax.random.normal(jax.random.fold_in(_rk, 9001), (2, 1), jnp.float32)
        _g = jnp.sign(_g) * jnp.maximum(jnp.abs(_g), 1.0) + (_g == 0) * 1.0
        g_xattn = _g[0]
        g_ffn = _g[1]
        return (x, ctx_1024, g_xattn, g_ffn)
    x, ctx_1024, g_xattn, g_ffn = _rec_inputs()

    def _L0_xattn_setup():
        import jax, jax.numpy as jnp
        import numpy as np
        DIM = 128
        HEADS = 16
        HEAD_DIM = DIM // HEADS
        SCALE = HEAD_DIM ** (-0.5)
        EPS = 1e-05

        def layer_norm(x, g, b):
            mu = jnp.mean(x, axis=-1, keepdims=True)
            var = jnp.mean(jnp.square(x - mu), axis=-1, keepdims=True)
            return (x - mu) * jax.lax.rsqrt(var + EPS) * g + b
        key = jax.random.key(seed)
        ks = jax.random.split(key, 8)
        B, Ls, Lt = (2, 256, 128)
        w_std = DIM ** (-0.5)
        return {'src': jax.random.normal(ks[0], (B, Ls, DIM), jnp.float32), 'tgt': jax.random.normal(ks[1], (B, Lt, DIM), jnp.float32), 'ln1_g': jnp.ones((DIM,), jnp.float32), 'ln1_b': jnp.zeros((DIM,), jnp.float32), 'ln2_g': jnp.ones((DIM,), jnp.float32), 'ln2_b': jnp.zeros((DIM,), jnp.float32), 'Wq': jax.random.normal(ks[2], (DIM, DIM), jnp.float32) * w_std, 'Wk': jax.random.normal(ks[3], (DIM, DIM), jnp.float32) * w_std, 'Wv': jax.random.normal(ks[4], (DIM, DIM), jnp.float32) * w_std, 'Wfc': jax.random.normal(ks[5], (DIM, DIM), jnp.float32) * w_std}
    _L0_xattn_all = _L0_xattn_setup()
    _L0_xattn_in = {k: v for k, v in _L0_xattn_all.items() if k in ('ln1_g', 'ln1_b', 'ln2_g', 'ln2_b', 'Wq', 'Wk', 'Wv', 'Wfc')}
    del _L0_xattn_all

    def _L0_ffn_setup():
        import jax, jax.numpy as jnp
        import numpy as np
        D_MODEL, FF_DIM = (128, 256)
        N_SHARED, N_ROUTED, TOP_K = (1, 8, 2)
        BATCH, SEQ = (2, 256)
        key = jax.random.key(seed)
        ks = jax.random.split(key, 8)
        init = lambda k, shape: jax.random.normal(k, shape, jnp.float32) * 0.02
        x = jax.random.normal(ks[0], (BATCH, SEQ, D_MODEL), jnp.float32)
        Wg = init(ks[1], (D_MODEL, N_ROUTED))
        Ws1 = init(ks[2], (D_MODEL, FF_DIM))
        Ws3 = init(ks[3], (D_MODEL, FF_DIM))
        Ws2 = init(ks[4], (FF_DIM, D_MODEL))
        We1 = init(ks[5], (N_ROUTED, D_MODEL, FF_DIM))
        We3 = init(ks[6], (N_ROUTED, D_MODEL, FF_DIM))
        We2 = init(ks[7], (N_ROUTED, FF_DIM, D_MODEL))
        return {'x': x, 'Wg': Wg, 'Ws1': Ws1, 'Ws3': Ws3, 'Ws2': Ws2, 'We1': We1, 'We3': We3, 'We2': We2}
    _L0_ffn_all = _L0_ffn_setup()
    _L0_ffn_in = {k: v for k, v in _L0_ffn_all.items() if k in ('Wg', 'Ws1', 'Ws3', 'Ws2', 'We1', 'We3', 'We2')}
    del _L0_ffn_all
    return {'x': x, 'ctx_1024': ctx_1024, 'g_xattn': g_xattn, 'g_ffn': g_ffn, 'L0_xattn_ln1_g': _L0_xattn_in['ln1_g'], 'L0_xattn_ln1_b': _L0_xattn_in['ln1_b'], 'L0_xattn_ln2_g': _L0_xattn_in['ln2_g'], 'L0_xattn_ln2_b': _L0_xattn_in['ln2_b'], 'L0_xattn_Wq': _L0_xattn_in['Wq'], 'L0_xattn_Wk': _L0_xattn_in['Wk'], 'L0_xattn_Wv': _L0_xattn_in['Wv'], 'L0_xattn_Wfc': _L0_xattn_in['Wfc'], 'L0_ffn_Wg': _L0_ffn_in['Wg'], 'L0_ffn_Ws1': _L0_ffn_in['Ws1'], 'L0_ffn_Ws3': _L0_ffn_in['Ws3'], 'L0_ffn_Ws2': _L0_ffn_in['Ws2'], 'L0_ffn_We1': _L0_ffn_in['We1'], 'L0_ffn_We3': _L0_ffn_in['We3'], 'L0_ffn_We2': _L0_ffn_in['We2']}

def reference(x, ctx_1024, g_xattn, g_ffn, L0_xattn_ln1_g, L0_xattn_ln1_b, L0_xattn_ln2_g, L0_xattn_ln2_b, L0_xattn_Wq, L0_xattn_Wk, L0_xattn_Wv, L0_xattn_Wfc, L0_ffn_Wg, L0_ffn_Ws1, L0_ffn_Ws3, L0_ffn_Ws2, L0_ffn_We1, L0_ffn_We3, L0_ffn_We2):
    import jax
    import jax.numpy as jnp

    def _L0_xattn_ref(src, tgt, ln1_g, ln1_b, ln2_g, ln2_b, Wq, Wk, Wv, Wfc):
        import jax, jax.numpy as jnp
        import numpy as np
        DIM = 128
        HEADS = 16
        HEAD_DIM = DIM // HEADS
        SCALE = HEAD_DIM ** (-0.5)
        EPS = 1e-05

        def layer_norm(x, g, b):
            mu = jnp.mean(x, axis=-1, keepdims=True)
            var = jnp.mean(jnp.square(x - mu), axis=-1, keepdims=True)
            return (x - mu) * jax.lax.rsqrt(var + EPS) * g + b
        B = src.shape[0]
        s = layer_norm(src, ln1_g, ln1_b)
        t = layer_norm(tgt, ln2_g, ln2_b)
        q = (t @ Wq).reshape(B, -1, HEADS, HEAD_DIM)
        k = (s @ Wk).reshape(B, -1, HEADS, HEAD_DIM)
        v = (s @ Wv).reshape(B, -1, HEADS, HEAD_DIM)
        attn = jnp.einsum('bqhd,bkhd->bhqk', q, k) * SCALE
        attn = jax.nn.softmax(attn, axis=-1)
        out = jnp.einsum('bhqk,bkhd->bqhd', attn, v).reshape(B, -1, DIM)
        return out @ Wfc

    def _L0_ffn_ref(x, Wg, Ws1, Ws3, Ws2, We1, We3, We2):
        import jax, jax.numpy as jnp
        import numpy as np
        D_MODEL, FF_DIM = (128, 256)
        N_SHARED, N_ROUTED, TOP_K = (1, 8, 2)
        BATCH, SEQ = (2, 256)
        B, S, d = x.shape
        E = Wg.shape[1]
        xf = x.reshape(-1, d)
        T = xf.shape[0]
        gates = jax.nn.sigmoid(xf @ Wg)
        vals, idx = jax.lax.top_k(gates, TOP_K)
        vals = vals / vals.sum(axis=-1, keepdims=True)
        w = jnp.zeros((T, E), x.dtype).at[jnp.arange(T)[:, None], idx].add(vals)
        shared = jax.nn.silu(xf @ Ws1) * (xf @ Ws3) @ Ws2
        h = jax.nn.silu(jnp.einsum('td,edf->tef', xf, We1)) * jnp.einsum('td,edf->tef', xf, We3)
        routed = jnp.einsum('tef,efd,te->td', h, We2, w)
        out = (shared + routed) / (N_SHARED + TOP_K)
        return out.reshape(B, S, d)
    x = x + jnp.tanh(g_xattn[0]) * _L0_xattn_ref(ctx_1024, _layernorm(x, axis=-1), L0_xattn_ln1_g, L0_xattn_ln1_b, L0_xattn_ln2_g, L0_xattn_ln2_b, L0_xattn_Wq, L0_xattn_Wk, L0_xattn_Wv, L0_xattn_Wfc)
    x = x + jnp.tanh(g_ffn[0]) * _L0_ffn_ref(_layernorm(x, axis=-1), L0_ffn_Wg, L0_ffn_Ws1, L0_ffn_Ws3, L0_ffn_Ws2, L0_ffn_We1, L0_ffn_We3, L0_ffn_We2)
    return x

_drawn_inputs = setup_inputs


def setup_inputs(seed=0):
    import zlib

    import numpy as np

    out = dict(_drawn_inputs(seed))
    spreads = {'L0_xattn_ln1_g': (1.0, 0.2),
     'L0_xattn_ln1_b': (0.0, 0.1),
     'L0_xattn_ln2_g': (1.0, 0.599),
     'L0_xattn_ln2_b': (0.0, 0.481)}
    factors = {'L0_ffn_Wg': 8.0,
     'L0_ffn_Ws1': 8.0,
     'L0_ffn_Ws3': 8.0,
     'L0_ffn_Ws2': 8.0,
     'L0_ffn_We1': 8.0,
     'L0_ffn_We3': 8.0,
     'L0_ffn_We2': 8.0}
    for name, (base, spread) in spreads.items():
        noise = np.random.default_rng([zlib.crc32(name.encode()), seed]).standard_normal(out[name].shape)
        drawn = base * np.exp(spread * noise) if base else spread * noise
        out[name] = jnp.asarray(drawn.astype(out[name].dtype))
    for name, factor in factors.items():
        out[name] = (out[name] * factor).astype(out[name].dtype)
    return out
```

```python
from contextlib import ExitStack

import concourse.bass as bass
from concourse import mybir

ALU = mybir.AluOpType
ACT = mybir.ActivationFunctionType
AX_X = mybir.AxisListType.X
F32 = mybir.dt.float32
F32R = mybir.dt.float32r

P = 128
EPS = 1e-5


def gated_attention_and_experts(nc, x, ctx_in, g_xattn, g_ffn, ln1_g, ln1_b, ln2_g, ln2_b,
                                wq, wk, wv, wfc, wg, ws1, ws3, ws2, we1, we3, we2, out):
    B, L, D = x.shape
    E, _, F = we1.shape
    HEADS = 16
    HD = D // HEADS
    SCALE = float(HD) ** -0.5
    NT = B * L // P
    HG = HEADS // 2
    CG = HG * HD
    NE = E + 1
    FH = F // P
    CH = 4
    NC = NT // CH
    CT = CH * P
    UP = 2 * F
    WUP = NE * UP
    WALL = WUP + NE * FH * D
    WSL = WALL // NT
    VW = 2 * HD + 2
    NHP = HEADS // 2
    assert B % 2 == 0 and L == 64 and D == P and WALL % NT == 0 and NC % 2 == 0

    xt = x.rearrange("(t b) l d -> (b l) t d", b=2)
    ct = ctx_in.rearrange("(t b) l d -> (b l) t d", b=2)
    ot = out.rearrange("(t b) l d -> (b l) t d", b=2)

    with ExitStack() as stack:
        def sb(name, shape, dt=F32):
            return stack.enter_context(nc.sbuf_tensor(name, shape, dt))

        def sem(name):
            return stack.enter_context(nc.semaphore(name))

        x_sb = sb("x_sb", [P, NT, D])
        c_sb = sb("c_sb", [P, NT, D])
        w_raw = sb("w_raw", [P, WALL])
        w_hi = sb("w_hi", [P, WALL], F32R)
        w_lo = sb("w_lo", [P, WALL], F32R)
        xT_hi = sb("xT_hi", [P, NC, CT], F32R)
        xT_lo = sb("xT_lo", [P, NC, CT], F32R)
        wq_sb = sb("wq_sb", [P, D])
        wk_sb = sb("wk_sb", [P, D])
        wv_sb = sb("wv_sb", [P, D])
        wfc_sb = sb("wfc_sb", [P, D])
        wg_raw = sb("wg_raw", [P, E])
        wg_hi = sb("wg_hi", [P, E], F32R)
        wg_lo = sb("wg_lo", [P, E], F32R)
        ln_sb = sb("ln_sb", [P, 4])
        gate_raw = sb("gate_raw", [P, 2])
        gate = sb("gate", [P, 2])
        gate3 = sb("gate3", [P, 1])
        ident = sb("ident", [P, P])
        head_ab = sb("head_ab", [P, 2, HG])
        head_mask = sb("head_mask", [P, HG])
        stats = sb("stats", [P, 2, 6])
        mv = sb("mv", [P, 2, 2, 2])
        var_eps = sb("var_eps", [P, 2])
        var_x = sb("var_x", [P, 1])
        var_x_eps = sb("var_x_eps", [P, 1])
        rstd_x = sb("rstd_x", [P, 1])
        scale_in = sb("scale_in", [P, 2, 2])
        var2_eps = sb("var2_eps", [P, 1])
        minus_half = sb("minus_half", [P, 2])
        eps = sb("eps", [P, 2])
        norm = sb("norm", [P, 2, 2, D])
        sT = sb("sT", [P, 2, D])
        tT = sb("tT", [P, 2, D])
        k_st = sb("k_st", [P, 2, 2, L])
        k_mask = sb("k_mask", [P, 2, 2, HG, L])
        q_blk = sb("q_blk", [P, 2, 2, P])
        v_mov = sb("v_mov", [P, 2, NHP, 2, VW])
        row_max = sb("row_max", [P, 2, HEADS])
        prob = sb("prob", [P, 2, HEADS, L])
        probT = sb("probT", [P, 2, NHP, P])
        inv_sum = sb("inv_sum", [P, NHP, 2])
        attn = sb("attn", [P, 2, D])
        attnT = sb("attnT", [P, 2, D])
        stats2 = sb("stats2", [P, 6])
        mv2 = sb("mv2", [P, 2, 2])
        rs2 = sb("rs2", [P, 2])
        xn2 = sb("xn2", [P, 2, D])
        gt = sb("gt", [P, NT, E])
        gt2 = sb("gt2", [P, NT, E])
        pick1 = sb("pick1", [P, NT, E])
        pick2 = sb("pick2", [P, NT, E])
        key = sb("key", [P, NT, E])
        order = sb("order", [P, E])
        top1 = sb("top1", [P, NT])
        top2 = sb("top2", [P, NT])
        rank = sb("rank", [P, NT])
        share = sb("share", [P, NT])
        wgt = sb("wgt", [P, NT, NE])
        sg = c_sb[:, 0:FH * CH, :].rearrange("p (f c) d -> p f (c d)", f=FH)
        h = c_sb[:, FH * CH:2 * FH * CH, :].rearrange("p (f c) d -> p f (c d)", f=FH)
        h_hi = sb("h_hi", [P, 2, FH, CT], F32R)
        h_lo = sb("h_lo", [P, 2, FH, CT], F32R)

        ps = stack.enter_context(nc.psum_tensor("ps", [P, 8, 512], F32))
        p_in = ps[:, 0, 0:2 * D].rearrange("p (a d) -> p a d", a=2)
        p_kq = ps[:, 1, 0:4 * L].rearrange("p (a l) -> p a l", a=4)
        p_v = ps[:, 1, 256:256 + 2 * CG].rearrange("p (a h d) -> p a h d", a=2, d=HD)
        p_s = ps[:, 2:4, :].rearrange("p g (h k) -> p (g h) k", k=L)
        p_pT = ps[:, 4:6, :]
        p_o = ps[:, 6, 0:NHP * 2 * VW].rearrange("p (h b v) -> p h b v", h=NHP, b=2)
        p_out = ps[:, 7, 0:D]

        x_in = [sem(f"x_in{i}") for i in range(4)]
        c_in = [sem(f"c_in{i}") for i in range(4)]
        w_in = sem("w_in")
        small_in = sem("small_in")
        w_all_in = sem("w_all_in")
        out_done = sem("out_done")
        ident_zero = sem("ident_zero")
        consts_ready = sem("consts_ready")
        mask_step = sem("mask_step")
        mask_ready = sem("mask_ready")
        v_static = sem("v_static")
        gate_ready = sem("gate_ready")
        gate3_ready = sem("gate3_ready")
        stats_done = sem("stats_done")
        aggr_done = sem("aggr_done")
        scale_step = sem("scale_step")
        scale_ready = sem("scale_ready")
        var2_done = sem("var2_done")
        norm_ready = sem("norm_ready")
        norm_turned = sem("norm_turned")
        sT_ready = sem("sT_ready")
        kqv_ready = sem("kqv_ready")
        k_out = sem("k_out")
        kqv_out = sem("kqv_out")
        k_masked = sem("k_masked")
        s_ready = sem("s_ready")
        max_done = sem("max_done")
        s_shifted = sem("s_shifted")
        exp_done = sem("exp_done")
        prob_turned = sem("prob_turned")
        probT_a = sem("probT_a")
        probT_b = sem("probT_b")
        o_ready = sem("o_ready")
        inv_done = sem("inv_done")
        attn_ready = sem("attn_ready")
        attn_turned = sem("attn_turned")
        attnT_ready = sem("attnT_ready")
        fc_ready = sem("fc_ready")
        x2_ready = sem("x2_ready")
        stats2_done = sem("stats2_done")
        aggr2_done = sem("aggr2_done")
        rs2_done = sem("rs2_done")
        xn2_ready = sem("xn2_ready")
        xn2_turned = sem("xn2_turned")
        xT_hi_ready = sem("xT_hi_ready")
        xT_lo_ready = sem("xT_lo_ready")
        w_hi_ready = sem("w_hi_ready")
        w_split = sem("w_split")
        wg_hi_ready = sem("wg_hi_ready")
        wg_split = sem("wg_split")
        logits_ready = sem("logits_ready")
        gate_exp = sem("gate_exp")
        route = sem("route")
        g_ready = sem("g_ready")
        u_ready = sem("u_ready")
        silu_done = sem("silu_done")
        h_done = sem("h_done")
        h_hi_done = sem("h_hi_done")
        h_lo_done = sem("h_lo_done")
        y_ready = sem("y_ready")
        acc_done = sem("acc_done")

        block = stack.enter_context(nc.Block())

        FIRST, LAST = -3, NT + 3
        LOOP_FROM = 4
        LOOP_TO = LOOP_FROM + 2 * ((NT - 3 - LOOP_FROM) // 2)

        def attention_steps(eng, step):
            for t in range(FIRST, LOOP_FROM):
                step(t, t % 2)
            with eng.Fori(0, (LOOP_TO - LOOP_FROM) // 2) as j:
                for u in range(2):
                    step(j * 2 + (LOOP_FROM + u), (LOOP_FROM + u) % 2)
            for t in range(LOOP_TO, LAST + 1):
                step(t, t % 2)

        def within(i):
            return not isinstance(i, int) or 0 <= i < NT

        def reused(i, n=2):
            return not isinstance(i, int) or i >= n

        UNITS = 2 * NE

        def expert_units(eng, first, unit):
            first()
            with eng.Fori(0, NC // 2 - 1) as j:
                for n in range(UNITS):
                    unit(j, n, True)
            for n in range(UNITS):
                unit(NC // 2 - 1, n, n < UNITS - 1)

        def chunk_of(j, n):
            return j * 2 + n // NE

        def w_up(w, e, which, f):
            at = e * UP + which * F + f * P
            return w[:, at:at + P]

        def w_down(w, e, f):
            at = WUP + (e * FH + f) * D
            return w[:, at:at + D]

        def xT_tile(t, i):
            flat = t[:, :, :].rearrange("p c t -> p (c t)")
            return flat[:, i * P:(i + 1) * P] if isinstance(i, int) else flat[:, bass.ts(i, P)]

        @block.sync
        def _(sp):
            q = NT // 4
            sp.dma_start(c_sb[:, 0:q, :], ct[:, 0:q, :]).then_inc(c_in[0], 16)
            sp.dma_start(x_sb[:, 0:q, :], xt[:, 0:q, :]).then_inc(x_in[0], 16)
            for k in range(1, 4):
                sp.dma_start(c_sb[:, k * q:(k + 1) * q, :], ct[:, k * q:(k + 1) * q, :]).then_inc(c_in[k], 16)
                sp.dma_start(x_sb[:, k * q:(k + 1) * q, :], xt[:, k * q:(k + 1) * q, :]).then_inc(x_in[k], 16)
            up = w_raw[:, 0:WUP].rearrange("p (e w f) -> p e w f", e=NE, w=2)
            down = w_raw[:, WUP:WALL].rearrange("p (e d) -> p e d", e=NE * FH)
            sp.dma_start(up[:, 0:E, 0, :], we1.rearrange("e d f -> d e f")).then_inc(w_all_in, 16)
            sp.dma_start(up[:, 0:E, 1, :], we3.rearrange("e d f -> d e f")).then_inc(w_all_in, 16)
            sp.dma_start(up[:, E, 0, :], ws1).then_inc(w_all_in, 16)
            sp.dma_start(up[:, E, 1, :], ws3).then_inc(w_all_in, 16)
            sp.dma_start(down[:, 0:E * FH, :], we2.rearrange("e (h f) d -> f (e h) d", f=P)).then_inc(w_all_in, 16)
            sp.dma_start(down[:, E * FH:NE * FH, :], ws2.rearrange("(h f) d -> f h d", f=P)).then_inc(w_all_in, 16)
            with sp.Fori(0, NC) as c:
                sp.wait_ge(acc_done, (c + 1) * (NE * CH))
                sp.dma_start(ot[:, bass.ts(c, CH), :], x_sb[:, bass.ts(c, CH), :]).then_inc(out_done, 16)
            sp.wait_ge(out_done, 16 * NC)

        @block.gpsimd
        def _(pool):
            pool.memset(ident[:, :], 0.0).then_inc(ident_zero, 1)
            pool.memset(head_ab[:, :, :], 1.0).then_inc(mask_step, 1)
            pool.wait_ge(ident_zero, 1)
            pool.affine_select(out=ident[:, :], in_=ident[:, :], compare_op=ALU.not_equal, fill=1.0, base=0,
                               pattern=[[-1, P]], channel_multiplier=1).then_inc(consts_ready, 1)
            pool.wait_ge(mask_step, 1)
            pool.affine_select(out=head_ab[:, :, :], in_=head_ab[:, :, :], compare_op=ALU.is_ge, fill=0.0, base=0,
                               pattern=[[-CG, 2], [-HD, HG]], channel_multiplier=1).then_inc(mask_step, 1)
            pool.wait_ge(mask_step, 2)
            pool.affine_select(out=head_ab[:, :, :], in_=head_ab[:, :, :], compare_op=ALU.is_ge, fill=0.0,
                               base=HD - 1, pattern=[[CG, 2], [HD, HG]], channel_multiplier=-1).then_inc(mask_step, 1)
            pool.wait_ge(mask_step, 3)
            pool.tensor_tensor(head_mask[:, :], head_ab[:, 0, :], head_ab[:, 1, :], ALU.add).then_inc(mask_ready, 1)
            pool.wait_ge(mask_ready, 1)
            for e in range(E):
                i = pool.memset(order[:, e:e + 1], float(E - e))
            i.then_inc(consts_ready, 1)
            pool.memset(minus_half[:, :], -0.5)
            pool.memset(eps[:, :], EPS).then_inc(scale_step, 1)
            pool.wait_ge(scale_step, 1)
            SC = 6

            def step(t, b):
                i = t + 3
                m = 1 - b
                if within(i):
                    pool.wait_ge(aggr_done, i + 1)
                    if reused(i):
                        pool.wait_ge(norm_ready, i - 1)
                    at = i * SC + 1
                    pool.tensor_tensor(var_eps[:, :], mv[:, m, :, 1], eps[:, :], ALU.add).then_inc(scale_step, 1)
                    pool.wait_ge(scale_step, at + 1)
                    pool.tensor_tensor(scale_in[:, m, :], var_eps[:, :], minus_half[:, :],
                                       ALU.pow).then_inc(scale_step, 1)
                    pool.wait_ge(scale_step, at + 2)
                    one = scale_in[:, m, 1:2]
                    pool.tensor_tensor(var_x[:, :], mv[:, m, 1, 1:2], one, ALU.mult).then_inc(scale_step, 1)
                    pool.wait_ge(scale_step, at + 3)
                    pool.tensor_tensor(var_x[:, :], var_x[:, :], one, ALU.mult).then_inc(scale_step, 1)
                    pool.wait_ge(scale_step, at + 4)
                    pool.tensor_tensor(var_x_eps[:, :], var_x[:, :], eps[:, 0:1], ALU.add).then_inc(scale_step, 1)
                    pool.wait_ge(scale_step, at + 5)
                    pool.tensor_tensor(rstd_x[:, :], var_x_eps[:, :], minus_half[:, 0:1],
                                       ALU.pow).then_inc(scale_step, 1)
                    pool.wait_ge(scale_step, at + 6)
                    pool.tensor_tensor(one, rstd_x[:, :], one, ALU.mult).then_inc(scale_ready, 1)
                    pool.wait_ge(scale_ready, i + 1)
                i = t - 2
                if within(i):
                    pool.wait_ge(aggr2_done, i + 1)
                    pool.tensor_tensor(var2_eps[:, :], mv2[:, b, 1:2], eps[:, 0:1], ALU.add).then_inc(var2_done, 1)
                    pool.wait_ge(var2_done, i + 1)
                    if reused(i):
                        pool.wait_ge(xn2_ready, i - 1)
                    pool.tensor_tensor(rs2[:, b:b + 1], var2_eps[:, :], minus_half[:, 0:1],
                                       ALU.pow).then_inc(rs2_done, 1)
                    pool.wait_ge(rs2_done, i + 1)
                i = t + 1
                if within(i):
                    pool.wait_ge(k_out, i + 1)
                    if reused(i):
                        pool.wait_ge(s_ready, i - 1)
                    shape = [P, 2, HG, L]
                    pool.tensor_tensor(k_mask[:, m, :, :, :],
                                       k_st[:, m, :, :].unsqueeze(2).broadcast_to(shape),
                                       head_mask[:, :].unsqueeze(1).unsqueeze(3).broadcast_to(shape),
                                       ALU.mult).then_inc(k_masked, 1)
                if within(t):
                    if isinstance(t, int) and t == 0:
                        pool.wait_ge(w_all_in, 96)
                    s = slice(t * WSL, (t + 1) * WSL) if isinstance(t, int) else bass.ts(t, WSL)
                    pool.tensor_copy(w_hi[:, s], w_raw[:, s]).then_inc(w_hi_ready, 1)
                    pool.wait_ge(w_hi_ready, t + 1)
                    pool.tensor_tensor(w_lo[:, s], w_raw[:, s], w_hi[:, s].bitcast(F32),
                                       ALU.subtract).then_inc(w_split, 1)

            attention_steps(pool, step)

            def low(j, n, f):
                u = j * UNITS + n
                m = n % 2
                pool.wait_ge(h_hi_done, u * FH + f + 1)
                pool.tensor_tensor(h_lo[:, m, f, :], h[:, f, :], h_hi[:, m, f, :].bitcast(F32),
                                   ALU.subtract).then_inc(h_lo_done, 1)

            def unit(j, n, more):
                if more:
                    for f in range(FH):
                        low(j, n + 1, f)

            expert_units(pool, lambda: [low(0, 0, f) for f in range(FH)], unit)

        @block.scalar
        def _(act):
            for t, src in ((wq_sb, wq), (wk_sb, wk), (wv_sb, wv), (wfc_sb, wfc)):
                act.dma_start(t[:, :], src).then_inc(w_in, 16)
            for k, src in enumerate((ln1_g, ln1_b, ln2_g, ln2_b)):
                act.dma_start(ln_sb[:, k:k + 1], src.rearrange("(d a) -> d a", a=1)).then_inc(small_in, 16)
            for k, src in enumerate((g_xattn, g_ffn)):
                act.dma_start(gate_raw[:, k:k + 1], src.partition_broadcast(P)).then_inc(small_in, 16)
            act.dma_start(wg_raw[:, :], wg).then_inc(small_in, 16)
            act.wait_ge(small_in, 16 * 7)
            act.activation(gate[:, :], gate_raw[:, :], ACT.Tanh).then_inc(gate_ready, 1)

            def step(t, b):
                i = t - 2
                if within(i):
                    act.wait_ge(attn_turned, i + 1)
                    if reused(i):
                        act.wait_ge(fc_ready, i - 1)
                    act.activation(attnT[:, b, :], p_out, ACT.Copy).then_inc(attnT_ready, 1)
                i = t + 1
                m = 1 - b
                if within(i):
                    act.wait_ge(norm_turned, i + 1)
                    if reused(i):
                        act.wait_ge(kqv_ready, i - 1)
                    act.activation(sT[:, m, :], p_in[:, 0, :], ACT.Identity, bias=ln_sb[:, 1:2], scale=ln_sb[:, 0:1])
                    act.activation(tT[:, m, :], p_in[:, 1, :], ACT.Identity, bias=ln_sb[:, 3:4],
                                   scale=ln_sb[:, 2:3]).then_inc(sT_ready, 1)
                i = t - 1
                if within(i):
                    act.wait_ge(prob_turned, i + 1)
                    if reused(i):
                        act.wait_ge(o_ready, i - 1)
                    act.activation(probT[:, m, 0:NHP // 2, :].rearrange("p h q -> p (h q)"), p_pT[:, 0, :],
                                   ACT.Copy).then_inc(probT_a, 1)
                i = t + 1
                if within(i):
                    act.wait_ge(kqv_ready, i + 1)
                    if reused(i):
                        act.wait_ge(k_masked, i - 1)
                        act.wait_ge(s_ready, i - 1)
                        act.wait_ge(o_ready, i - 1)
                    act.activation(k_st[:, m, :, :], p_kq[:, 0:2, :], ACT.Copy).then_inc(k_out, 1)
                    if isinstance(i, int) and i == 0:
                        act.wait_ge(v_static, 1)
                    for s in range(2):
                        r = slice(L * s, L * s + L)
                        act.activation(q_blk[r, m, :, r], p_kq[r, 2:4, :], ACT.Copy)
                    for s in range(2):
                        r = slice(L * s, L * s + L)
                        last = act.activation(v_mov[r, m, :, :, HD * s:HD * s + HD],
                                              p_v[r, :, :, :].rearrange("p a h d -> p h a d"), ACT.Copy)
                    last.then_inc(kqv_out, 1)
                if within(t):
                    act.wait_ge(s_shifted, t + 1)
                    act.activation(prob[:, b, :, :], prob[:, b, :, :], ACT.Exp, scale=SCALE).then_inc(exp_done, 1)
                i = t - 4
                if within(i):
                    act.wait_ge(xn2_turned, i + 1)
                    act.activation(xT_tile(xT_hi, i), p_out, ACT.Copy).then_inc(xT_hi_ready, 1)

            attention_steps(act, step)
            act.wait_ge(logits_ready, 1)
            act.activation(gt[:, :, :], ps[:, 6, 0:NT * E].rearrange("p (t e) -> p t e", e=E), ACT.Exp,
                           scale=-1.0).then_inc(gate_exp, 1)

            def hidden(j, n):
                u = j * UNITS + n
                m = n % 2
                first = isinstance(j, int) and j == 0
                for f in range(FH):
                    act.wait_ge(g_ready, u * FH + f + 1)
                    if not (first and n == 0):
                        act.wait_ge(h_done, (u - 1) * FH + f + 1)
                    act.activation(sg[:, f, :], ps[:, 2 * f, :], ACT.Silu).then_inc(silu_done, 1)
                for f in range(FH):
                    act.wait_ge(h_done, u * FH + f + 1)
                    if not (first and n < 2):
                        act.wait_ge(y_ready, u - 1)
                    act.activation(h_hi[:, m, f, :], h[:, f, :], ACT.Copy).then_inc(h_hi_done, 1)

            def unit(j, n, more):
                if more:
                    hidden(j, n + 1)

            expert_units(act, lambda: hidden(0, 0), unit)

        @block.vector
        def _(dve):
            dve.memset(q_blk[:, :, :, :], 0.0)
            dve.memset(v_mov[:, :, :, :, :], 0.0).then_inc(v_static, 1)
            dve.wait_ge(v_static, 1)
            dve.memset(v_mov[0:L, :, :, :, 2 * HD:2 * HD + 1], 1.0)
            dve.memset(v_mov[L:P, :, :, :, 2 * HD + 1:2 * HD + 2], 1.0).then_inc(v_static, 1)

            def step(t, b):
                m = 1 - b
                i = t + 3
                if within(i):
                    if reused(i, 1):
                        dve.wait_ge(aggr_done, i)
                    if reused(i):
                        dve.wait_ge(norm_ready, i - 1)
                i = t - 2
                if within(i):
                    if reused(i, 1):
                        dve.wait_ge(aggr2_done, i)
                    if reused(i):
                        dve.wait_ge(xn2_ready, i - 1)
                if within(t):
                    dve.wait_ge(s_ready, t + 1)
                    if reused(t):
                        dve.wait_ge(prob_turned, t - 1)
                    dve.tensor_reduce(row_max[:, b, :], p_s, AX_X, ALU.max).then_inc(max_done, 1)
                    dve.wait_ge(max_done, t + 1)
                    dve.tensor_tensor(prob[:, b, :, :], p_s,
                                      row_max[:, b, :].unsqueeze(2).broadcast_to([P, HEADS, L]),
                                      ALU.subtract).then_inc(s_shifted, 1)
                i = t - 1
                if within(i):
                    dve.wait_ge(prob_turned, i + 1)
                    if reused(i):
                        dve.wait_ge(o_ready, i - 1)
                    dve.tensor_copy(probT[:, m, NHP // 2:NHP, :].rearrange("p h q -> p (h q)"),
                                    p_pT[:, 1, :]).then_inc(probT_b, 1)
                i = t - 2
                if within(i):
                    dve.wait_ge(fc_ready, i + 1)
                    if isinstance(i, int) and i == 0:
                        dve.wait_ge(gate_ready, 1)
                    dve.scalar_tensor_tensor(out=x_sb[:, i, :], in0=p_out, scalar=gate[:, 0:1], in1=x_sb[:, i, :],
                                             op0=ALU.mult, op1=ALU.add).then_inc(x2_ready, 1)
                    dve.wait_ge(x2_ready, i + 1)
                i = t - 3
                if within(i):
                    dve.wait_ge(rs2_done, i + 1)
                    if reused(i):
                        dve.wait_ge(xn2_turned, i - 1)
                    dve.tensor_scalar(xn2[:, m, :], x_sb[:, i, :], mv2[:, m, 0:1], rs2[:, m:m + 1], ALU.subtract,
                                      ALU.mult).then_inc(xn2_ready, 1)
                i = t - 2
                if within(i):
                    dve.bn_stats(stats2[:, :], x_sb[:, i, :]).then_inc(stats2_done, 1)
                i = t + 3
                if within(i):
                    if isinstance(i, int) and i == 0:
                        dve.wait_ge(c_in[0], 16)
                        dve.wait_ge(x_in[0], 16)
                    if isinstance(i, int) and i == LOOP_FROM + 2:
                        for k in range(1, 4):
                            dve.wait_ge(c_in[k], 16)
                            dve.wait_ge(x_in[k], 16)
                    dve.bn_stats(stats[:, 0, :], c_sb[:, i, :])
                    dve.bn_stats(stats[:, 1, :], x_sb[:, i, :]).then_inc(stats_done, 1)
                if within(t - 2):
                    dve.wait_ge(stats2_done, t - 1)
                if within(t + 3):
                    dve.wait_ge(stats_done, t + 4)
                i = t - 1
                if within(i):
                    dve.wait_ge(o_ready, i + 1)
                    for s in range(2):
                        r = slice(L * s, L * s + L)
                        last = dve.reciprocal(inv_sum[r, :, :], p_o[r, :, s, 2 * HD:VW])
                    last.then_inc(inv_done, 1)
                if within(t - 2):
                    dve.bn_aggr(mv2[:, b, :], stats2[:, :]).then_inc(aggr2_done, 1)
                if within(t + 3):
                    dve.bn_aggr(mv[:, m, 0, :], stats[:, 0, :])
                    dve.bn_aggr(mv[:, m, 1, :], stats[:, 1, :]).then_inc(aggr_done, 1)
                if within(i):
                    dve.wait_ge(inv_done, i + 1)
                    if reused(i):
                        dve.wait_ge(attn_turned, i - 1)
                    for s in range(2):
                        r = slice(L * s, L * s + L)
                        last = dve.tensor_tensor(
                            attn[r, m, :].rearrange("p (h s d) -> p h s d", s=2, d=HD),
                            p_o[r, :, s, 0:2 * HD].rearrange("p h (s d) -> p h s d", s=2),
                            inv_sum[r, :, :].unsqueeze(3).broadcast_to([L, NHP, 2, HD]), ALU.mult)
                    last.then_inc(attn_ready, 1)
                i = t - 4
                if within(i):
                    dve.wait_ge(xT_hi_ready, i + 1)
                    dve.tensor_tensor(xT_tile(xT_lo, i), p_out, xT_tile(xT_hi, i).bitcast(F32),
                                      ALU.subtract).then_inc(xT_lo_ready, 1)
                i = t + 2
                if within(i):
                    dve.wait_ge(scale_ready, i + 1)
                    if reused(i):
                        dve.wait_ge(norm_turned, i - 1)
                    dve.tensor_scalar(norm[:, b, 0, :], c_sb[:, i, :], mv[:, b, 0, 0:1], scale_in[:, b, 0:1],
                                      ALU.subtract, ALU.mult)
                    dve.tensor_scalar(norm[:, b, 1, :], x_sb[:, i, :], mv[:, b, 1, 0:1], scale_in[:, b, 1:2],
                                      ALU.subtract, ALU.mult).then_inc(norm_ready, 1)

            attention_steps(dve, step)
            dve.tensor_copy(wg_hi[:, :], wg_raw[:, :]).then_inc(wg_hi_ready, 1)
            dve.wait_ge(wg_hi_ready, 1)
            dve.tensor_tensor(wg_lo[:, :], wg_raw[:, :], wg_hi[:, :].bitcast(F32), ALU.subtract).then_inc(wg_split, 1)
            count = [0]

            def then(instruction):
                count[0] += 1
                instruction.then_inc(route, 1)
                dve.wait_ge(route, count[0])

            full = [P, NT, E]

            def spread(v):
                return v[:, :].unsqueeze(2).broadcast_to(full)

            then(dve.tensor_scalar(gate3[:, :], gate[:, 1:2], 1.0 / 3.0, None, ALU.mult))
            dve.wait_ge(gate_exp, 1)
            then(dve.tensor_scalar(gt[:, :, :], gt[:, :, :], 1.0, None, ALU.add))
            then(dve.reciprocal(gt[:, :, :], gt[:, :, :]))
            late = order[:, :].unsqueeze(1).broadcast_to(full)
            dve.wait_ge(consts_ready, 2)
            for scores, top, pick in ((gt, top1, pick1), (gt2, top2, pick2)):
                then(dve.tensor_reduce(top[:, :], scores[:, :, :], AX_X, ALU.max))
                then(dve.tensor_tensor(key[:, :, :], scores[:, :, :], spread(top), ALU.is_equal))
                then(dve.tensor_tensor(key[:, :, :], key[:, :, :], late, ALU.mult))
                then(dve.tensor_reduce(rank[:, :], key[:, :, :], AX_X, ALU.max))
                then(dve.tensor_tensor(pick[:, :, :], key[:, :, :], spread(rank), ALU.is_equal))
                if pick is pick1:
                    then(dve.scalar_tensor_tensor(out=gt2[:, :, :], in0=pick[:, :, :], scalar=-4.0, in1=gt[:, :, :],
                                                  op0=ALU.mult, op1=ALU.add))
            then(dve.tensor_tensor(share[:, :], top1[:, :], top2[:, :], ALU.add))
            then(dve.reciprocal(share[:, :], share[:, :]))
            then(dve.tensor_scalar(share[:, :], share[:, :], gate3[:, 0:1], None, ALU.mult))
            then(dve.tensor_tensor(top1[:, :], top1[:, :], share[:, :], ALU.mult))
            then(dve.tensor_tensor(top2[:, :], top2[:, :], share[:, :], ALU.mult))
            then(dve.tensor_tensor(pick1[:, :, :], pick1[:, :, :], spread(top1), ALU.mult))
            then(dve.tensor_tensor(pick2[:, :, :], pick2[:, :, :], spread(top2), ALU.mult))
            dve.tensor_copy(wgt[:, :, E:NE], gate3[:, 0:1].unsqueeze(1).broadcast_to([P, NT, 1]))
            then(dve.tensor_tensor(wgt[:, :, 0:E], pick1[:, :, :], pick2[:, :, :], ALU.add))

            def hidden(j, n):
                u = j * UNITS + n
                first = isinstance(j, int) and j == 0
                for f in range(FH):
                    dve.wait_ge(u_ready, u * FH + f + 1)
                    dve.wait_ge(silu_done, u * FH + f + 1)
                    if not (first and n == 0):
                        dve.wait_ge(h_lo_done, (u - 1) * FH + f + 1)
                    dve.tensor_tensor(h[:, f, :], ps[:, 2 * f + 1, :], sg[:, f, :], ALU.mult).then_inc(h_done, 1)

            def unit(j, n, more):
                if more:
                    hidden(j, n + 1)
                u = j * UNITS + n
                c = chunk_of(j, n)
                e = n % NE
                dve.wait_ge(y_ready, u + 1)
                if not (isinstance(j, int) and j == 0 and n == 0):
                    dve.wait_ge(acc_done, u * CH)
                for k in range(CH):
                    i = c * CH + k
                    dve.scalar_tensor_tensor(out=x_sb[:, i, :], in0=ps[:, 4 + n % 2, k * D:(k + 1) * D],
                                             scalar=wgt[:, i, e:e + 1], in1=x_sb[:, i, :], op0=ALU.mult,
                                             op1=ALU.add).then_inc(acc_done, 1)

            expert_units(dve, lambda: hidden(0, 0), unit)

        @block.tensor
        def _(pe):
            pe.wait_ge(consts_ready, 1)
            pe.wait_ge(w_in, 64)

            def step(t, b):
                m = 1 - b
                if within(t):
                    pe.wait_ge(kqv_out, t + 1)
                    pe.wait_ge(k_masked, t + 1)
                    if reused(t, 1):
                        pe.wait_ge(s_shifted, t)
                    for g in range(2):
                        last = pe.matmul(ps[:, 2 + g, :], q_blk[:, b, g, :],
                                         k_mask[:, b, g, :, :].rearrange("p h k -> p (h k)"), start=True, stop=True)
                    last.then_inc(s_ready, 1)
                i = t - 2
                if within(i):
                    pe.wait_ge(attn_ready, i + 1)
                    if reused(i, 3):
                        pe.wait_ge(xT_lo_ready, i - 2)
                    pe.transpose(p_out, attn[:, b, :], ident[:, :]).then_inc(attn_turned, 1)
                i = t + 1
                if within(i):
                    pe.wait_ge(norm_ready, i + 1)
                    if reused(i, 1):
                        pe.wait_ge(sT_ready, i)
                    pe.transpose(p_in[:, 0, :], norm[:, m, 0, :], ident[:, :])
                    pe.transpose(p_in[:, 1, :], norm[:, m, 1, :], ident[:, :]).then_inc(norm_turned, 1)
                i = t - 1
                if within(i):
                    pe.wait_ge(exp_done, i + 1)
                    if reused(i, 1):
                        pe.wait_ge(probT_a, i)
                        pe.wait_ge(probT_b, i)
                    flat = prob[:, m, :, :].rearrange("p h k -> p (h k)")
                    for hp in range(NHP):
                        last = pe.transpose(ps[:, 4 + hp // 4, (hp % 4) * P:(hp % 4 + 1) * P],
                                            flat[:, hp * P:(hp + 1) * P], ident[:, :])
                    last.then_inc(prob_turned, 1)
                i = t - 2
                if within(i):
                    pe.wait_ge(attnT_ready, i + 1)
                    pe.matmul(p_out, attnT[:, b, :], wfc_sb[:, :], start=True, stop=True).then_inc(fc_ready, 1)
                i = t + 1
                if within(i):
                    pe.wait_ge(sT_ready, i + 1)
                    if reused(i, 1):
                        pe.wait_ge(kqv_out, i)
                    for which, w, src in ((0, wk_sb, sT), (1, wq_sb, tT)):
                        for g in range(2):
                            for s in range(2):
                                pe.matmul(p_kq[L * s:L * s + L, 2 * which + g, :], w[:, g * CG:(g + 1) * CG],
                                          src[:, m, L * s:L * s + L], start=True, stop=True)
                    for s in range(2):
                        for o in range(2):
                            last = pe.matmul(p_v[L * o:L * o + L, s, :, :], sT[:, m, L * s:L * s + L],
                                             wv_sb[:, :].rearrange("p (h o d) -> p o h d", o=2, d=HD)[:, o, :, :],
                                             start=True, stop=True)
                    last.then_inc(kqv_ready, 1)
                i = t - 1
                if within(i):
                    pe.wait_ge(probT_a, i + 1)
                    pe.wait_ge(probT_b, i + 1)
                    if reused(i, 1):
                        pe.wait_ge(attn_ready, i)
                    for hp in range(NHP):
                        last = pe.matmul(p_o[:, hp, :, :].rearrange("p b v -> p (b v)"), probT[:, m, hp, :],
                                         v_mov[:, m, hp, :, :].rearrange("p b v -> p (b v)"), start=True, stop=True)
                    last.then_inc(o_ready, 1)
                i = t - 4
                if within(i):
                    pe.wait_ge(xn2_ready, i + 1)
                    if within(i + 2):
                        pe.wait_ge(x2_ready, i + 3)
                    else:
                        pe.wait_ge(xT_lo_ready, i)
                    pe.transpose(p_out, xn2[:, b, :], ident[:, :]).then_inc(xn2_turned, 1)

            attention_steps(pe, step)
            pe.wait_ge(xT_lo_ready, NT)
            pe.wait_ge(wg_split, 1)
            pe.wait_ge(attn_ready, NT)
            for i in range(NT):
                o = ps[:, 6, i * E:(i + 1) * E]
                pe.matmul(o, xT_tile(xT_hi, i), wg_hi[:, :], start=True, stop=False)
                pe.matmul(o, xT_tile(xT_lo, i), wg_hi[:, :], start=False, stop=False)
                last = pe.matmul(o, xT_tile(xT_hi, i), wg_lo[:, :], start=False, stop=True)
            last.then_inc(logits_ready, 1)
            pe.wait_ge(w_split, NT)
            pe.wait_ge(s_shifted, NT)

            def up(j, n):
                u = j * UNITS + n
                c = chunk_of(j, n)
                e = n % NE
                first = isinstance(j, int) and j == 0
                for f in range(FH):
                    for which, done, free in ((0, g_ready, silu_done), (1, u_ready, h_done)):
                        if not (first and n == 0):
                            pe.wait_ge(free, (u - 1) * FH + f + 1)
                        o = ps[:, 2 * f + which, :]
                        pe.matmul(o, w_up(w_hi, e, which, f), xT_hi[:, c, :], start=True, stop=False)
                        pe.matmul(o, w_up(w_hi, e, which, f), xT_lo[:, c, :], start=False, stop=False)
                        pe.matmul(o, w_up(w_lo, e, which, f), xT_hi[:, c, :], start=False, stop=True).then_inc(done, 1)

            def unit(j, n, more):
                if more:
                    up(j, n + 1)
                u = j * UNITS + n
                e = n % NE
                m = n % 2
                first = isinstance(j, int) and j == 0
                pe.wait_ge(h_lo_done, (u + 1) * FH)
                if n == 0:
                    pe.wait_ge(acc_done, u * CH)
                elif not (first and n < 2):
                    pe.wait_ge(acc_done, (u - 1) * CH)
                for k in range(CH):
                    o = ps[:, 4 + m, k * D:(k + 1) * D]
                    for f in range(FH):
                        hi = h_hi[:, m, f, k * P:(k + 1) * P]
                        lo = h_lo[:, m, f, k * P:(k + 1) * P]
                        pe.matmul(o, hi, w_down(w_hi, e, f), start=(f == 0), stop=False)
                        pe.matmul(o, hi, w_down(w_lo, e, f), start=False, stop=False)
                        last = pe.matmul(o, lo, w_down(w_hi, e, f), start=False, stop=(f == FH - 1))
                last.then_inc(y_ready, 1)

            expert_units(pe, lambda: up(0, 0), unit)


_INS = ['x', 'ctx_1024', 'g_xattn', 'g_ffn', 'L0_xattn_ln1_g', 'L0_xattn_ln1_b', 'L0_xattn_ln2_g', 'L0_xattn_ln2_b',
        'L0_xattn_Wq', 'L0_xattn_Wk', 'L0_xattn_Wv', 'L0_xattn_Wfc', 'L0_ffn_Wg', 'L0_ffn_Ws1', 'L0_ffn_Ws3',
        'L0_ffn_Ws2', 'L0_ffn_We1', 'L0_ffn_We3', 'L0_ffn_We2']
_OUTS = [((64, 64, 128), 'float32')]


def kernel(**inputs):
    import numpy as _np
    import concourse.bacc as _bacc
    from concourse import mybir as _mybir
    from concourse.bass_utils import run_bass_kernel_spmd as _run

    nc = _bacc.Bacc("TRN2", target_bir_lowering=False, num_devices=1)
    arrays, args = {}, []
    for name in _INS:
        a = _np.ascontiguousarray(inputs[name])
        arrays[f"in_{name}_dram"] = a
        args.append(nc.dram_tensor(f"in_{name}_dram", a.shape, _mybir.dt.from_np(a.dtype), kind="ExternalInput").ap())
    for i, (shape, dtype) in enumerate(_OUTS):
        dt = _mybir.dt.from_np(_np.dtype(dtype))
        args.append(nc.dram_tensor(f"out_{i}_dram", shape, dt, kind="ExternalOutput").ap())
    gated_attention_and_experts(nc, *args)
    r = _run(nc, [arrays], core_ids=[0])
    got = tuple(r.results[0][f"out_{i}_dram"] for i in range(len(_OUTS)))
    return got[0]
```

```python
from contextlib import ExitStack

import concourse.bass as bass
from concourse import mybir

ALU = mybir.AluOpType
ACT = mybir.ActivationFunctionType
AX_X = mybir.AxisListType.X
F32 = mybir.dt.float32
F32R = mybir.dt.float32r

P = 128
EPS = 1e-5


def gated_attention_and_experts(nc, x, ctx_in, g_xattn, g_ffn, ln1_g, ln1_b, ln2_g, ln2_b,
                                wq, wk, wv, wfc, wg, ws1, ws3, ws2, we1, we3, we2, out):
    B, L, D = x.shape
    E, _, F = we1.shape
    HEADS = 16
    HD = D // HEADS
    SCALE = float(HD) ** -0.5
    NT = B * L // P
    HG = HEADS // 2
    CG = HG * HD
    NE = E + 1
    FH = F // P
    CH = 4
    NC = NT // CH
    CT = CH * P
    UP = 2 * F
    WUP = NE * UP
    WALL = WUP + NE * FH * D
    WSL = WALL // NT
    VW = 2 * HD + 2
    NHP = HEADS // 2
    assert B % 2 == 0 and L == 64 and D == P and WALL % NT == 0 and NC % 2 == 0

    xt = x.rearrange("(t b) l d -> (b l) t d", b=2)
    ct = ctx_in.rearrange("(t b) l d -> (b l) t d", b=2)
    ot = out.rearrange("(t b) l d -> (b l) t d", b=2)

    with ExitStack() as stack:
        def sb(name, shape, dt=F32):
            return stack.enter_context(nc.sbuf_tensor(name, shape, dt))

        def sem(name):
            return stack.enter_context(nc.semaphore(name))

        x_sb = sb("x_sb", [P, NT, D])
        c_sb = sb("c_sb", [P, NT, D])
        w_raw = sb("w_raw", [P, WALL])
        w_hi = sb("w_hi", [P, WALL], F32R)
        w_lo = sb("w_lo", [P, WALL], F32R)
        xT_hi = sb("xT_hi", [P, NC, CT], F32R)
        xT_lo = sb("xT_lo", [P, NC, CT], F32R)
        wq_sb = sb("wq_sb", [P, D])
        wk_sb = sb("wk_sb", [P, D])
        wv_sb = sb("wv_sb", [P, D])
        wfc_sb = sb("wfc_sb", [P, D])
        wg_raw = sb("wg_raw", [P, E])
        wg_hi = sb("wg_hi", [P, E], F32R)
        wg_lo = sb("wg_lo", [P, E], F32R)
        ln_sb = sb("ln_sb", [P, 4])
        gate_raw = sb("gate_raw", [P, 2])
        gate = sb("gate", [P, 2])
        gate3 = sb("gate3", [P, 1])
        ident = sb("ident", [P, P])
        head_ab = sb("head_ab", [P, 2, HG])
        head_mask = sb("head_mask", [P, HG])
        stats = sb("stats", [P, 2, 6])
        mv = sb("mv", [P, 2, 2, 2])
        var_eps = sb("var_eps", [P, 2])
        var_x = sb("var_x", [P, 1])
        var_b_eps = sb("var_b_eps", [P, 2])
        rstd_b = sb("rstd_b", [P, 2, 2])
        scale_in = sb("scale_in", [P, 2, 2])
        minus_half = sb("minus_half", [P, 2])
        eps = sb("eps", [P, 2])
        norm = sb("norm", [P, 2, 2, D])
        sT = sb("sT", [P, 2, D])
        tT = sb("tT", [P, 2, D])
        k_st = sb("k_st", [P, 2, 2, L])
        k_mask = sb("k_mask", [P, 2, 2, HG, L])
        q_blk = sb("q_blk", [P, 2, 2, P])
        v_mov = sb("v_mov", [P, 2, NHP, 2, VW])
        row_max = sb("row_max", [P, 2, HEADS])
        prob = sb("prob", [P, 2, HEADS, L])
        probT = sb("probT", [P, 2, NHP, P])
        inv_sum = sb("inv_sum", [P, NHP, 2])
        attn = sb("attn", [P, 2, D])
        attnT = sb("attnT", [P, 2, D])
        stats2 = sb("stats2", [P, 6])
        mv2 = sb("mv2", [P, 2, 2])
        xT_f32 = sb("xT_f32", [P, 2, D])
        xn2 = sb("xn2", [P, 2, D])
        order = sb("order", [P, E])
        top1 = sb("top1", [P, NT])
        top2 = sb("top2", [P, NT])
        rank = sb("rank", [P, NT])
        share = sb("share", [P, NT])
        wgt = sb("wgt", [P, NT, NE])
        sg = c_sb[:, 0:FH * CH, :].rearrange("p (f c) d -> p f (c d)", f=FH)
        h = c_sb[:, FH * CH:2 * FH * CH, :].rearrange("p (f c) d -> p f (c d)", f=FH)
        gt, gt2, pick1, pick2, key = (
            c_sb[:, k:k + 2, :].rearrange("p a (t e) -> p (a t) e", e=E) for k in range(2 * FH * CH, 2 * FH * CH + 10, 2))
        h_hi = sb("h_hi", [P, 2, FH, CT], F32R)
        h_lo = sb("h_lo", [P, 2, FH, CT], F32R)

        ps = stack.enter_context(nc.psum_tensor("ps", [P, 8, 512], F32))
        p_in = ps[:, 0, 0:2 * D].rearrange("p (a d) -> p a d", a=2)
        p_x2 = ps[:, 0, 2 * D:3 * D]
        p_kq = ps[:, 1, 0:4 * L].rearrange("p (a l) -> p a l", a=4)
        p_v = ps[:, 1, 256:256 + 2 * CG].rearrange("p (a h d) -> p a h d", a=2, d=HD)
        p_s = ps[:, 2:4, :].rearrange("p g (h k) -> p (g h) k", k=L)
        p_pT = ps[:, 4:6, :]
        p_o = ps[:, 6, 0:NHP * 2 * VW].rearrange("p (h b v) -> p h b v", h=NHP, b=2)
        p_out = ps[:, 7, 0:D]

        x_in = [sem(f"x_in{i}") for i in range(4)]
        c_in = [sem(f"c_in{i}") for i in range(4)]
        w_in = sem("w_in")
        small_in = sem("small_in")
        w_all_in = sem("w_all_in")
        out_done = sem("out_done")
        ident_zero = sem("ident_zero")
        consts_ready = sem("consts_ready")
        mask_step = sem("mask_step")
        mask_ready = sem("mask_ready")
        v_static = sem("v_static")
        gate_ready = sem("gate_ready")
        gate3_ready = sem("gate3_ready")
        stats_done = sem("stats_done")
        aggr_done = sem("aggr_done")
        scale_step = sem("scale_step")
        scale_ready = sem("scale_ready")
        var2_done = sem("var2_done")
        tail_step = sem("tail_step")
        norm_ready = sem("norm_ready")
        norm_turned = sem("norm_turned")
        sT_ready = sem("sT_ready")
        kqv_ready = sem("kqv_ready")
        k_out = sem("k_out")
        q_out = sem("q_out")
        v_out = sem("v_out")
        k_masked = sem("k_masked")
        s_ready = sem("s_ready")
        max_done = sem("max_done")
        s_shifted = sem("s_shifted")
        exp_done = sem("exp_done")
        prob_turned = sem("prob_turned")
        probT_done = sem("probT_done")
        o_ready = sem("o_ready")
        inv_done = sem("inv_done")
        attn_ready = sem("attn_ready")
        attn_turned = sem("attn_turned")
        attnT_ready = sem("attnT_ready")
        fc_ready = sem("fc_ready")
        x2_ready = sem("x2_ready")
        stats2_done = sem("stats2_done")
        aggr2_done = sem("aggr2_done")
        xT_f32_ready = sem("xT_f32_ready")
        xn2_ready = sem("xn2_ready")
        xn2_turned = sem("xn2_turned")
        xT_hi_ready = sem("xT_hi_ready")
        xT_lo_ready = sem("xT_lo_ready")
        w_hi_ready = sem("w_hi_ready")
        w_split = sem("w_split")
        wg_hi_ready = sem("wg_hi_ready")
        wg_split = sem("wg_split")
        logits_ready = sem("logits_ready")
        gate_exp = sem("gate_exp")
        route = sem("route")
        g_ready = sem("g_ready")
        u_ready = sem("u_ready")
        silu_done = sem("silu_done")
        h_done = sem("h_done")
        h_hi_done = sem("h_hi_done")
        h_lo_done = sem("h_lo_done")
        y_ready = sem("y_ready")
        acc_done = sem("acc_done")

        block = stack.enter_context(nc.Block())

        FIRST, LAST = -3, NT + 4
        LOOP_FROM = 6
        LOOP_TO = LOOP_FROM + 2 * ((NT - 3 - LOOP_FROM) // 2)

        def attention_steps(eng, step):
            for t in range(FIRST, LOOP_FROM):
                step(t, t % 2)
            with eng.Fori(0, (LOOP_TO - LOOP_FROM) // 2) as j:
                for u in range(2):
                    step(j * 2 + (LOOP_FROM + u), (LOOP_FROM + u) % 2)
            for t in range(LOOP_TO, LAST + 1):
                step(t, t % 2)

        def within(i):
            return not isinstance(i, int) or 0 <= i < NT

        def reused(i, n=2):
            return not isinstance(i, int) or i >= n

        UNITS = 2 * NE

        def expert_units(eng, first, unit):
            first()
            with eng.Fori(0, NC // 2 - 1) as j:
                for n in range(UNITS):
                    unit(j, n, True)
            for n in range(UNITS):
                unit(NC // 2 - 1, n, n < UNITS - 1)

        def chunk_of(j, n):
            return j * 2 + n // NE

        def w_up(w, e, which, f):
            at = e * UP + which * F + f * P
            return w[:, at:at + P]

        def w_down(w, e, f):
            at = WUP + (e * FH + f) * D
            return w[:, at:at + D]

        def xT_tile(t, i):
            flat = t[:, :, :].rearrange("p c t -> p (c t)")
            return flat[:, i * P:(i + 1) * P] if isinstance(i, int) else flat[:, bass.ts(i, P)]

        def w_slice(t):
            return slice(t * WSL, (t + 1) * WSL) if isinstance(t, int) else bass.ts(t, WSL)

        @block.sync
        def _(sp):
            q = NT // 4
            sp.dma_start(c_sb[:, 0:q, :], ct[:, 0:q, :]).then_inc(c_in[0], 16)
            sp.dma_start(x_sb[:, 0:q, :], xt[:, 0:q, :]).then_inc(x_in[0], 16)
            for k in range(1, 4):
                sp.dma_start(c_sb[:, k * q:(k + 1) * q, :], ct[:, k * q:(k + 1) * q, :]).then_inc(c_in[k], 16)
                sp.dma_start(x_sb[:, k * q:(k + 1) * q, :], xt[:, k * q:(k + 1) * q, :]).then_inc(x_in[k], 16)
            up = w_raw[:, 0:WUP].rearrange("p (e w f) -> p e w f", e=NE, w=2)
            down = w_raw[:, WUP:WALL].rearrange("p (e d) -> p e d", e=NE * FH)
            sp.dma_start(up[:, 0:E, 0, :], we1.rearrange("e d f -> d e f")).then_inc(w_all_in, 16)
            sp.dma_start(up[:, 0:E, 1, :], we3.rearrange("e d f -> d e f")).then_inc(w_all_in, 16)
            sp.dma_start(up[:, E, 0, :], ws1).then_inc(w_all_in, 16)
            sp.dma_start(up[:, E, 1, :], ws3).then_inc(w_all_in, 16)
            sp.dma_start(down[:, 0:E * FH, :], we2.rearrange("e (h f) d -> f (e h) d", f=P)).then_inc(w_all_in, 16)
            sp.dma_start(down[:, E * FH:NE * FH, :], ws2.rearrange("(h f) d -> f h d", f=P)).then_inc(w_all_in, 16)
            with sp.Fori(0, NC) as c:
                sp.wait_ge(acc_done, (c + 1) * (NE * CH))
                sp.dma_start(ot[:, bass.ts(c, CH), :], x_sb[:, bass.ts(c, CH), :]).then_inc(out_done, 16)
            sp.wait_ge(out_done, 16 * NC)

        @block.gpsimd
        def _(pool):
            pool.memset(ident[:, :], 0.0).then_inc(ident_zero, 1)
            pool.memset(head_ab[:, :, :], 1.0).then_inc(mask_step, 1)
            pool.wait_ge(ident_zero, 1)
            pool.affine_select(out=ident[:, :], in_=ident[:, :], compare_op=ALU.not_equal, fill=1.0, base=0,
                               pattern=[[-1, P]], channel_multiplier=1).then_inc(consts_ready, 1)
            pool.wait_ge(mask_step, 1)
            pool.affine_select(out=head_ab[:, :, :], in_=head_ab[:, :, :], compare_op=ALU.is_ge, fill=0.0, base=0,
                               pattern=[[-CG, 2], [-HD, HG]], channel_multiplier=1).then_inc(mask_step, 1)
            pool.wait_ge(mask_step, 2)
            pool.affine_select(out=head_ab[:, :, :], in_=head_ab[:, :, :], compare_op=ALU.is_ge, fill=0.0,
                               base=HD - 1, pattern=[[CG, 2], [HD, HG]], channel_multiplier=-1).then_inc(mask_step, 1)
            pool.wait_ge(mask_step, 3)
            pool.tensor_tensor(head_mask[:, :], head_ab[:, 0, :], head_ab[:, 1, :], ALU.add).then_inc(mask_ready, 1)
            pool.wait_ge(mask_ready, 1)
            for e in range(E):
                i = pool.memset(order[:, e:e + 1], float(E - e))
            i.then_inc(consts_ready, 1)
            pool.memset(minus_half[:, :], -0.5)
            pool.memset(eps[:, :], EPS).then_inc(scale_step, 1)
            pool.wait_ge(scale_step, 1)
            SC = 6

            def step(t, b):
                m = 1 - b
                i = t + 2
                i2 = t - 4
                if within(i):
                    pool.wait_ge(aggr_done, i + 1)
                    if reused(i):
                        pool.wait_ge(norm_ready, i - 1)
                    at = i * SC + 1
                    one = scale_in[:, b, 1:2]
                    pool.tensor_tensor(var_eps[:, :], mv[:, b, :, 1], eps[:, :], ALU.add).then_inc(scale_step, 1)
                    pool.wait_ge(scale_step, at + 1)
                    pool.tensor_tensor(scale_in[:, b, :], var_eps[:, :], minus_half[:, :],
                                       ALU.pow).then_inc(scale_step, 1)
                    pool.wait_ge(scale_step, at + 2)
                    pool.tensor_tensor(var_x[:, :], mv[:, b, 1, 1:2], one, ALU.mult).then_inc(scale_step, 1)
                    pool.wait_ge(scale_step, at + 3)
                    pool.tensor_tensor(var_x[:, :], var_x[:, :], one, ALU.mult).then_inc(scale_step, 1)
                    pool.wait_ge(scale_step, at + 4)
                    pool.tensor_tensor(var_b_eps[:, 0:1], var_x[:, :], eps[:, 0:1], ALU.add).then_inc(scale_step, 1)
                if within(i2):
                    pool.wait_ge(aggr2_done, i2 + 1)
                    pool.tensor_tensor(var_b_eps[:, 1:2], mv2[:, b, 1:2], eps[:, 0:1], ALU.add).then_inc(var2_done, 1)
                    pool.wait_ge(var2_done, i2 + 1)
                if within(i):
                    pool.wait_ge(scale_step, at + 5)
                    cols = slice(0, 2 if within(i2) else 1)
                    if within(i2) and reused(i2):
                        pool.wait_ge(xn2_ready, i2 - 1)
                    pool.tensor_tensor(rstd_b[:, b, cols], var_b_eps[:, cols], minus_half[:, cols],
                                       ALU.pow).then_inc(scale_step, 1)
                    pool.wait_ge(scale_step, at + 6)
                    pool.tensor_tensor(one, rstd_b[:, b, 0:1], one, ALU.mult).then_inc(scale_ready, 1)
                    pool.wait_ge(scale_ready, i + 1)
                elif within(i2):
                    if reused(i2):
                        pool.wait_ge(xn2_ready, i2 - 1)
                    pool.tensor_tensor(rstd_b[:, b, 1:2], var_b_eps[:, 1:2], minus_half[:, 1:2],
                                       ALU.pow).then_inc(tail_step, 1)
                    pool.wait_ge(tail_step, i2 - (NT - 6) + 1)
                i = t + 1
                if within(i):
                    pool.wait_ge(k_out, i + 1)
                    if reused(i):
                        pool.wait_ge(s_ready, i - 1)
                    shape = [P, 2, HG, L]
                    pool.tensor_tensor(k_mask[:, m, :, :, :],
                                       k_st[:, m, :, :].unsqueeze(2).broadcast_to(shape),
                                       head_mask[:, :].unsqueeze(1).unsqueeze(3).broadcast_to(shape),
                                       ALU.mult).then_inc(k_masked, 1)
                i = t - 5
                if within(i):
                    pool.wait_ge(xT_f32_ready, i + 1)
                    pool.tensor_tensor(xT_tile(xT_lo, i), xT_f32[:, m, :], xT_tile(xT_hi, i).bitcast(F32),
                                       ALU.subtract).then_inc(xT_lo_ready, 1)
                if within(t):
                    pool.wait_ge(w_hi_ready, t + 1)
                    s = w_slice(t)
                    pool.tensor_tensor(w_lo[:, s], w_raw[:, s], w_hi[:, s].bitcast(F32),
                                       ALU.subtract).then_inc(w_split, 1)

            attention_steps(pool, step)

            def low(j, n, f):
                u = j * UNITS + n
                m = n % 2
                pool.wait_ge(h_hi_done, u * FH + f + 1)
                pool.tensor_tensor(h_lo[:, m, f, :], h[:, f, :], h_hi[:, m, f, :].bitcast(F32),
                                   ALU.subtract).then_inc(h_lo_done, 1)

            def unit(j, n, more):
                if more:
                    for f in range(FH):
                        low(j, n + 1, f)

            expert_units(pool, lambda: [low(0, 0, f) for f in range(FH)], unit)

        @block.scalar
        def _(act):
            for t, src in ((wq_sb, wq), (wk_sb, wk), (wv_sb, wv), (wfc_sb, wfc)):
                act.dma_start(t[:, :], src).then_inc(w_in, 16)
            for k, src in enumerate((ln1_g, ln1_b, ln2_g, ln2_b)):
                act.dma_start(ln_sb[:, k:k + 1], src.rearrange("(d a) -> d a", a=1)).then_inc(small_in, 16)
            for k, src in enumerate((g_xattn, g_ffn)):
                act.dma_start(gate_raw[:, k:k + 1], src.partition_broadcast(P)).then_inc(small_in, 16)
            act.dma_start(wg_raw[:, :], wg).then_inc(small_in, 16)
            act.wait_ge(small_in, 16 * 7)
            act.activation(gate[:, :], gate_raw[:, :], ACT.Tanh).then_inc(gate_ready, 1)

            def step(t, b):
                m = 1 - b
                i = t - 1
                if within(i):
                    act.wait_ge(s_shifted, i + 1)
                    act.activation(prob[:, m, :, :], prob[:, m, :, :], ACT.Exp, scale=SCALE).then_inc(exp_done, 1)
                if within(t):
                    if isinstance(t, int) and t == 0:
                        act.wait_ge(v_static, 2)
                    if reused(t):
                        act.wait_ge(o_ready, t - 1)
                    for s in range(2):
                        r = slice(L * s, L * s + L)
                        last = act.activation(v_mov[r, b, :, :, HD * s:HD * s + HD],
                                              p_v[r, :, :, :].rearrange("p a h d -> p h a d"), ACT.Copy)
                    last.then_inc(v_out, 1)
                i = t + 1
                if within(i):
                    act.wait_ge(norm_turned, i + 1)
                    if reused(i):
                        act.wait_ge(kqv_ready, i - 1)
                    act.activation(sT[:, m, :], p_in[:, 0, :], ACT.Identity, bias=ln_sb[:, 1:2], scale=ln_sb[:, 0:1])
                    act.activation(tT[:, m, :], p_in[:, 1, :], ACT.Identity, bias=ln_sb[:, 3:4],
                                   scale=ln_sb[:, 2:3]).then_inc(sT_ready, 1)
                i = t - 2
                if within(i):
                    act.wait_ge(attn_turned, i + 1)
                    if reused(i):
                        act.wait_ge(fc_ready, i - 1)
                    act.activation(attnT[:, b, :], p_out, ACT.Copy).then_inc(attnT_ready, 1)
                i = t + 1
                if within(i):
                    act.wait_ge(kqv_ready, i + 1)
                    if reused(i):
                        act.wait_ge(k_masked, i - 1)
                        act.wait_ge(s_ready, i - 1)
                    act.activation(k_st[:, m, :, :], p_kq[:, 0:2, :], ACT.Copy).then_inc(k_out, 1)
                    if isinstance(i, int) and i == 0:
                        act.wait_ge(v_static, 1)
                    for s in range(2):
                        r = slice(L * s, L * s + L)
                        last = act.activation(q_blk[r, m, :, r], p_kq[r, 2:4, :], ACT.Copy)
                    last.then_inc(q_out, 1)
                i = t - 1
                if within(i):
                    for half in range(2):
                        act.wait_ge(prob_turned, i * 2 + half + 1)
                        if reused(i) and half == 0:
                            act.wait_ge(o_ready, i - 1)
                        act.activation(probT[:, m, half * NHP // 2:(half + 1) * NHP // 2, :].rearrange("p h q -> p (h q)"),
                                       p_pT[:, half, :], ACT.Copy).then_inc(probT_done, 1)
                i = t - 5
                if within(i):
                    act.wait_ge(xn2_turned, i + 1)
                    act.activation(xT_tile(xT_hi, i), p_x2, ACT.Copy)
                    if reused(i):
                        act.wait_ge(xT_lo_ready, i - 1)
                    act.activation(xT_f32[:, m, :], p_x2, ACT.Copy).then_inc(xT_f32_ready, 1)
                if within(t):
                    if isinstance(t, int) and t == 0:
                        act.wait_ge(w_all_in, 96)
                    s = w_slice(t)
                    act.activation(w_hi[:, s], w_raw[:, s], ACT.Copy).then_inc(w_hi_ready, 1)

            attention_steps(act, step)
            act.wait_ge(logits_ready, 1)
            act.activation(gt[:, :, :], ps[:, 6, 0:NT * E].rearrange("p (t e) -> p t e", e=E), ACT.Exp,
                           scale=-1.0).then_inc(gate_exp, 1)

            def hidden(j, n):
                u = j * UNITS + n
                m = n % 2
                first = isinstance(j, int) and j == 0
                for f in range(FH):
                    act.wait_ge(g_ready, u * FH + f + 1)
                    if not (first and n == 0):
                        act.wait_ge(h_done, (u - 1) * FH + f + 1)
                    act.activation(sg[:, f, :], ps[:, 2 * f, :], ACT.Silu).then_inc(silu_done, 1)
                for f in range(FH):
                    act.wait_ge(h_done, u * FH + f + 1)
                    if not (first and n < 2):
                        act.wait_ge(y_ready, u - 1)
                    act.activation(h_hi[:, m, f, :], h[:, f, :], ACT.Copy).then_inc(h_hi_done, 1)

            def unit(j, n, more):
                if more:
                    hidden(j, n + 1)

            expert_units(act, lambda: hidden(0, 0), unit)

        @block.vector
        def _(dve):
            dve.memset(q_blk[:, :, :, :], 0.0)
            dve.memset(v_mov[:, :, :, :, :], 0.0).then_inc(v_static, 1)
            dve.wait_ge(v_static, 1)
            dve.memset(v_mov[0:L, :, :, :, 2 * HD:2 * HD + 1], 1.0)
            dve.memset(v_mov[L:P, :, :, :, 2 * HD + 1:2 * HD + 2], 1.0).then_inc(v_static, 1)

            def step(t, b):
                m = 1 - b
                if within(t + 3):
                    if reused(t + 3, 1):
                        dve.wait_ge(aggr_done, t + 3)
                    if reused(t + 3):
                        dve.wait_ge(norm_ready, t + 2)
                i = t - 3
                if within(i):
                    if reused(i, 1):
                        dve.wait_ge(aggr2_done, i)
                    dve.wait_ge(fc_ready, i + 1)
                    if isinstance(i, int) and i == 0:
                        dve.wait_ge(gate_ready, 1)
                    dve.scalar_tensor_tensor(out=x_sb[:, i, :], in0=p_out, scalar=gate[:, 0:1], in1=x_sb[:, i, :],
                                             op0=ALU.mult, op1=ALU.add).then_inc(x2_ready, 1)
                if within(t):
                    dve.wait_ge(s_ready, t + 1)
                    if reused(t):
                        dve.wait_ge(prob_turned, (t - 1) * 2)
                    dve.tensor_reduce(row_max[:, b, :], p_s, AX_X, ALU.max).then_inc(max_done, 1)
                    dve.wait_ge(max_done, t + 1)
                    if within(i):
                        dve.wait_ge(x2_ready, i + 1)
                    dve.tensor_tensor(prob[:, b, :, :], p_s,
                                      row_max[:, b, :].unsqueeze(2).broadcast_to([P, HEADS, L]),
                                      ALU.subtract).then_inc(s_shifted, 1)
                elif within(i):
                    dve.wait_ge(x2_ready, i + 1)
                if within(i):
                    dve.bn_stats(stats2[:, :], x_sb[:, i, :]).then_inc(stats2_done, 1)
                i = t + 3
                if within(i):
                    if isinstance(i, int) and i == 0:
                        dve.wait_ge(c_in[0], 16)
                        dve.wait_ge(x_in[0], 16)
                    if isinstance(i, int) and i == LOOP_FROM + 2:
                        for k in range(1, 4):
                            dve.wait_ge(c_in[k], 16)
                            dve.wait_ge(x_in[k], 16)
                    dve.bn_stats(stats[:, 0, :], c_sb[:, i, :])
                    dve.bn_stats(stats[:, 1, :], x_sb[:, i, :]).then_inc(stats_done, 1)
                i = t + 2
                if within(i):
                    dve.wait_ge(scale_ready, i + 1)
                    if reused(i):
                        dve.wait_ge(norm_turned, i - 1)
                    dve.tensor_scalar(norm[:, b, 0, :], c_sb[:, i, :], mv[:, b, 0, 0:1], scale_in[:, b, 0:1],
                                      ALU.subtract, ALU.mult)
                    dve.tensor_scalar(norm[:, b, 1, :], x_sb[:, i, :], mv[:, b, 1, 0:1], scale_in[:, b, 1:2],
                                      ALU.subtract, ALU.mult).then_inc(norm_ready, 1)
                i = t - 4
                if within(i):
                    if within(t + 2):
                        dve.wait_ge(scale_ready, t + 3)
                    else:
                        dve.wait_ge(tail_step, i - (NT - 6) + 1)
                    if reused(i):
                        dve.wait_ge(xn2_turned, i - 1)
                    dve.tensor_scalar(xn2[:, b, :], x_sb[:, i, :], mv2[:, b, 0:1], rstd_b[:, b, 1:2], ALU.subtract,
                                      ALU.mult).then_inc(xn2_ready, 1)
                if within(t - 3):
                    dve.wait_ge(stats2_done, t - 2)
                    if reused(t - 3):
                        dve.wait_ge(xn2_ready, t - 4)
                if within(t + 3):
                    dve.wait_ge(stats_done, t + 4)
                i = t - 1
                if within(i):
                    dve.wait_ge(o_ready, i + 1)
                    for s in range(2):
                        r = slice(L * s, L * s + L)
                        last = dve.reciprocal(inv_sum[r, :, :], p_o[r, :, s, 2 * HD:VW])
                    last.then_inc(inv_done, 1)
                if within(t - 3):
                    dve.bn_aggr(mv2[:, m, :], stats2[:, :]).then_inc(aggr2_done, 1)
                if within(t + 3):
                    dve.bn_aggr(mv[:, m, 0, :], stats[:, 0, :])
                    dve.bn_aggr(mv[:, m, 1, :], stats[:, 1, :]).then_inc(aggr_done, 1)
                if within(i):
                    dve.wait_ge(inv_done, i + 1)
                    if reused(i):
                        dve.wait_ge(attn_turned, i - 1)
                    for s in range(2):
                        r = slice(L * s, L * s + L)
                        last = dve.tensor_tensor(
                            attn[r, m, :].rearrange("p (h s d) -> p h s d", s=2, d=HD),
                            p_o[r, :, s, 0:2 * HD].rearrange("p h (s d) -> p h s d", s=2),
                            inv_sum[r, :, :].unsqueeze(3).broadcast_to([L, NHP, 2, HD]), ALU.mult)
                    last.then_inc(attn_ready, 1)

            attention_steps(dve, step)
            dve.tensor_copy(wg_hi[:, :], wg_raw[:, :]).then_inc(wg_hi_ready, 1)
            dve.wait_ge(wg_hi_ready, 1)
            dve.tensor_tensor(wg_lo[:, :], wg_raw[:, :], wg_hi[:, :].bitcast(F32), ALU.subtract).then_inc(wg_split, 1)
            count = [0]

            def then(instruction):
                count[0] += 1
                instruction.then_inc(route, 1)
                dve.wait_ge(route, count[0])

            full = [P, NT, E]

            def spread(v):
                return v[:, :].unsqueeze(2).broadcast_to(full)

            then(dve.tensor_scalar(gate3[:, :], gate[:, 1:2], 1.0 / 3.0, None, ALU.mult))
            dve.wait_ge(gate_exp, 1)
            then(dve.tensor_scalar(gt[:, :, :], gt[:, :, :], 1.0, None, ALU.add))
            then(dve.reciprocal(gt[:, :, :], gt[:, :, :]))
            late = order[:, :].unsqueeze(1).broadcast_to(full)
            dve.wait_ge(consts_ready, 2)
            for scores, top, pick in ((gt, top1, pick1), (gt2, top2, pick2)):
                then(dve.tensor_reduce(top[:, :], scores[:, :, :], AX_X, ALU.max))
                then(dve.tensor_tensor(key[:, :, :], scores[:, :, :], spread(top), ALU.is_equal))
                then(dve.tensor_tensor(key[:, :, :], key[:, :, :], late, ALU.mult))
                then(dve.tensor_reduce(rank[:, :], key[:, :, :], AX_X, ALU.max))
                then(dve.tensor_tensor(pick[:, :, :], key[:, :, :], spread(rank), ALU.is_equal))
                if pick is pick1:
                    then(dve.scalar_tensor_tensor(out=gt2[:, :, :], in0=pick[:, :, :], scalar=-4.0, in1=gt[:, :, :],
                                                  op0=ALU.mult, op1=ALU.add))
            then(dve.tensor_tensor(share[:, :], top1[:, :], top2[:, :], ALU.add))
            then(dve.reciprocal(share[:, :], share[:, :]))
            then(dve.tensor_scalar(share[:, :], share[:, :], gate3[:, 0:1], None, ALU.mult))
            then(dve.tensor_tensor(top1[:, :], top1[:, :], share[:, :], ALU.mult))
            then(dve.tensor_tensor(top2[:, :], top2[:, :], share[:, :], ALU.mult))
            then(dve.tensor_tensor(pick1[:, :, :], pick1[:, :, :], spread(top1), ALU.mult))
            then(dve.tensor_tensor(pick2[:, :, :], pick2[:, :, :], spread(top2), ALU.mult))
            dve.tensor_copy(wgt[:, :, E:NE], gate3[:, 0:1].unsqueeze(1).broadcast_to([P, NT, 1]))
            then(dve.tensor_tensor(wgt[:, :, 0:E], pick1[:, :, :], pick2[:, :, :], ALU.add))

            def hidden(j, n):
                u = j * UNITS + n
                first = isinstance(j, int) and j == 0
                for f in range(FH):
                    dve.wait_ge(u_ready, u * FH + f + 1)
                    dve.wait_ge(silu_done, u * FH + f + 1)
                    if not (first and n == 0):
                        dve.wait_ge(h_lo_done, (u - 1) * FH + f + 1)
                    dve.tensor_tensor(h[:, f, :], ps[:, 2 * f + 1, :], sg[:, f, :], ALU.mult).then_inc(h_done, 1)

            def unit(j, n, more):
                if more:
                    hidden(j, n + 1)
                u = j * UNITS + n
                c = chunk_of(j, n)
                e = n % NE
                dve.wait_ge(y_ready, u + 1)
                if not (isinstance(j, int) and j == 0 and n == 0):
                    dve.wait_ge(acc_done, u * CH)
                for k in range(CH):
                    i = c * CH + k
                    dve.scalar_tensor_tensor(out=x_sb[:, i, :], in0=ps[:, 4 + n % 2, k * D:(k + 1) * D],
                                             scalar=wgt[:, i, e:e + 1], in1=x_sb[:, i, :], op0=ALU.mult,
                                             op1=ALU.add).then_inc(acc_done, 1)

            expert_units(dve, lambda: hidden(0, 0), unit)

        @block.tensor
        def _(pe):
            pe.wait_ge(consts_ready, 1)
            pe.wait_ge(w_in, 64)

            def step(t, b):
                m = 1 - b
                i = t + 1
                if within(i):
                    pe.wait_ge(norm_ready, i + 1)
                    if reused(i, 1):
                        pe.wait_ge(sT_ready, i)
                    if within(t - 6):
                        pe.wait_ge(xT_f32_ready, t - 5)
                    pe.transpose(p_in[:, 0, :], norm[:, m, 0, :], ident[:, :])
                    pe.transpose(p_in[:, 1, :], norm[:, m, 1, :], ident[:, :]).then_inc(norm_turned, 1)
                if within(t):
                    pe.wait_ge(q_out, t + 1)
                    pe.wait_ge(k_masked, t + 1)
                    if reused(t, 1):
                        pe.wait_ge(s_shifted, t)
                    for g in range(2):
                        last = pe.matmul(ps[:, 2 + g, :], q_blk[:, b, g, :],
                                         k_mask[:, b, g, :, :].rearrange("p h k -> p (h k)"), start=True, stop=True)
                    last.then_inc(s_ready, 1)
                i = t + 1
                if within(i):
                    pe.wait_ge(sT_ready, i + 1)
                    if reused(i, 1):
                        pe.wait_ge(v_out, i)
                    for which, w, src in ((0, wk_sb, sT), (1, wq_sb, tT)):
                        for g in range(2):
                            for s in range(2):
                                pe.matmul(p_kq[L * s:L * s + L, 2 * which + g, :], w[:, g * CG:(g + 1) * CG],
                                          src[:, m, L * s:L * s + L], start=True, stop=True)
                    for s in range(2):
                        for o in range(2):
                            last = pe.matmul(p_v[L * o:L * o + L, s, :, :], sT[:, m, L * s:L * s + L],
                                             wv_sb[:, :].rearrange("p (h o d) -> p o h d", o=2, d=HD)[:, o, :, :],
                                             start=True, stop=True)
                    last.then_inc(kqv_ready, 1)
                i = t - 2
                if within(i):
                    pe.wait_ge(attn_ready, i + 1)
                    if reused(i, 1):
                        pe.wait_ge(x2_ready, i)
                    pe.transpose(p_out, attn[:, b, :], ident[:, :]).then_inc(attn_turned, 1)
                i = t - 1
                if within(i):
                    pe.wait_ge(exp_done, i + 1)
                    flat = prob[:, m, :, :].rearrange("p h k -> p (h k)")
                    for half in range(2):
                        if reused(i, 1):
                            pe.wait_ge(probT_done, i * 2 - 1 + half)
                        for hp in range(half * NHP // 2, (half + 1) * NHP // 2):
                            last = pe.transpose(ps[:, 4 + half, (hp % 4) * P:(hp % 4 + 1) * P],
                                                flat[:, hp * P:(hp + 1) * P], ident[:, :])
                        last.then_inc(prob_turned, 1)
                i = t - 2
                if within(i):
                    pe.wait_ge(attnT_ready, i + 1)
                    pe.matmul(p_out, attnT[:, b, :], wfc_sb[:, :], start=True, stop=True).then_inc(fc_ready, 1)
                i = t - 5
                if within(i):
                    pe.wait_ge(xn2_ready, i + 1)
                    if not within(t + 1) and reused(i, 1):
                        pe.wait_ge(xT_f32_ready, i)
                    pe.transpose(p_x2, xn2[:, m, :], ident[:, :]).then_inc(xn2_turned, 1)
                i = t - 1
                if within(i):
                    pe.wait_ge(v_out, i + 1)
                    pe.wait_ge(probT_done, i * 2 + 2)
                    if reused(i, 1):
                        pe.wait_ge(attn_ready, i)
                    for hp in range(NHP):
                        last = pe.matmul(p_o[:, hp, :, :].rearrange("p b v -> p (b v)"), probT[:, m, hp, :],
                                         v_mov[:, m, hp, :, :].rearrange("p b v -> p (b v)"), start=True, stop=True)
                    last.then_inc(o_ready, 1)

            attention_steps(pe, step)
            pe.wait_ge(xT_lo_ready, NT)
            pe.wait_ge(wg_split, 1)
            pe.wait_ge(attn_ready, NT)
            for i in range(NT):
                o = ps[:, 6, i * E:(i + 1) * E]
                pe.matmul(o, xT_tile(xT_hi, i), wg_hi[:, :], start=True, stop=False)
                pe.matmul(o, xT_tile(xT_lo, i), wg_hi[:, :], start=False, stop=False)
                last = pe.matmul(o, xT_tile(xT_hi, i), wg_lo[:, :], start=False, stop=True)
            last.then_inc(logits_ready, 1)
            pe.wait_ge(w_split, NT)
            pe.wait_ge(s_shifted, NT)

            def up(j, n):
                u = j * UNITS + n
                c = chunk_of(j, n)
                e = n % NE
                first = isinstance(j, int) and j == 0
                for f in range(FH):
                    for which, done, free in ((0, g_ready, silu_done), (1, u_ready, h_done)):
                        if not (first and n == 0):
                            pe.wait_ge(free, (u - 1) * FH + f + 1)
                        o = ps[:, 2 * f + which, :]
                        pe.matmul(o, w_up(w_hi, e, which, f), xT_hi[:, c, :], start=True, stop=False)
                        pe.matmul(o, w_up(w_hi, e, which, f), xT_lo[:, c, :], start=False, stop=False)
                        pe.matmul(o, w_up(w_lo, e, which, f), xT_hi[:, c, :], start=False, stop=True).then_inc(done, 1)

            def unit(j, n, more):
                if more:
                    up(j, n + 1)
                u = j * UNITS + n
                e = n % NE
                m = n % 2
                first = isinstance(j, int) and j == 0
                pe.wait_ge(h_lo_done, (u + 1) * FH)
                if n == 0:
                    pe.wait_ge(acc_done, u * CH)
                elif not (first and n < 2):
                    pe.wait_ge(acc_done, (u - 1) * CH)
                for k in range(CH):
                    o = ps[:, 4 + m, k * D:(k + 1) * D]
                    for f in range(FH):
                        hi = h_hi[:, m, f, k * P:(k + 1) * P]
                        lo = h_lo[:, m, f, k * P:(k + 1) * P]
                        pe.matmul(o, hi, w_down(w_hi, e, f), start=(f == 0), stop=False)
                        pe.matmul(o, hi, w_down(w_lo, e, f), start=False, stop=False)
                        last = pe.matmul(o, lo, w_down(w_hi, e, f), start=False, stop=(f == FH - 1))
                last.then_inc(y_ready, 1)

            expert_units(pe, lambda: up(0, 0), unit)


_INS = ['x', 'ctx_1024', 'g_xattn', 'g_ffn', 'L0_xattn_ln1_g', 'L0_xattn_ln1_b', 'L0_xattn_ln2_g', 'L0_xattn_ln2_b',
        'L0_xattn_Wq', 'L0_xattn_Wk', 'L0_xattn_Wv', 'L0_xattn_Wfc', 'L0_ffn_Wg', 'L0_ffn_Ws1', 'L0_ffn_Ws3',
        'L0_ffn_Ws2', 'L0_ffn_We1', 'L0_ffn_We3', 'L0_ffn_We2']
_OUTS = [((64, 64, 128), 'float32')]


def kernel(**inputs):
    import numpy as _np
    import concourse.bacc as _bacc
    from concourse import mybir as _mybir
    from concourse.bass_utils import run_bass_kernel_spmd as _run

    nc = _bacc.Bacc("TRN2", target_bir_lowering=False, num_devices=1)
    arrays, args = {}, []
    for name in _INS:
        a = _np.ascontiguousarray(inputs[name])
        arrays[f"in_{name}_dram"] = a
        args.append(nc.dram_tensor(f"in_{name}_dram", a.shape, _mybir.dt.from_np(a.dtype), kind="ExternalInput").ap())
    for i, (shape, dtype) in enumerate(_OUTS):
        dt = _mybir.dt.from_np(_np.dtype(dtype))
        args.append(nc.dram_tensor(f"out_{i}_dram", shape, dt, kind="ExternalOutput").ap())
    gated_attention_and_experts(nc, *args)
    r = _run(nc, [arrays], core_ids=[0])
    got = tuple(r.results[0][f"out_{i}_dram"] for i in range(len(_OUTS)))
    return got[0]
```

```python
from contextlib import ExitStack

import concourse.bass as bass
from concourse import mybir

ALU = mybir.AluOpType
ACT = mybir.ActivationFunctionType
AX_X = mybir.AxisListType.X
F32 = mybir.dt.float32
F32R = mybir.dt.float32r

P = 128
EPS = 1e-5




def gated_attention_and_experts(nc, x, ctx_in, g_xattn, g_ffn, ln1_g, ln1_b, ln2_g, ln2_b,
                                wq, wk, wv, wfc, wg, ws1, ws3, ws2, we1, we3, we2, out, w_dram):
    B, L, D = x.shape
    E, _, F = we1.shape
    HEADS = 16
    HD = D // HEADS
    SCALE = float(HD) ** -0.5
    NT = B * L // P
    HG = HEADS // 2
    CG = HG * HD
    NE = E + 1
    FH = F // P
    CH = 4
    NC = NT // CH
    CT = CH * P
    UP = 2 * F
    WUP = NE * UP
    WALL = WUP + NE * FH * D
    WSL = 2 * P
    SPLITS = WALL // WSL
    WS_FROM = NT - 1 - SPLITS
    HT = NT // 2
    VW = 2 * HD + 2
    NHP = HEADS // 2
    assert B % 2 == 0 and L == 64 and D == P and WALL % WSL == 0 and 0 < WS_FROM < 6 and HT * E == P and NC % 2 == 0

    xt = x.rearrange("(t b) l d -> (b l) t d", b=2)
    ct = ctx_in.rearrange("(t b) l d -> (b l) t d", b=2)
    ot = out.rearrange("(t b) l d -> (b l) t d", b=2)

    with ExitStack() as stack:
        def sb(name, shape, dt=F32):
            return stack.enter_context(nc.sbuf_tensor(name, shape, dt))

        def sem(name):
            return stack.enter_context(nc.semaphore(name))

        x_sb = sb("x_sb", [P, NT, D])
        c_sb = sb("c_sb", [P, NT, D])
        w_raw = sb("w_raw", [P, WALL])
        w_hi = sb("w_hi", [P, WALL], F32R)
        w_lo = sb("w_lo", [P, WALL], F32R)
        xT_hi = sb("xT_hi", [P, NC, CT], F32R)
        xT_lo = sb("xT_lo", [P, NC, CT], F32R)
        wq_sb = sb("wq_sb", [P, D])
        wk_sb = sb("wk_sb", [P, D])
        wv_sb = sb("wv_sb", [P, D])
        wfc_sb = sb("wfc_sb", [P, D])
        wg_raw = sb("wg_raw", [P, E])
        ln_sb = sb("ln_sb", [P, 4])
        gate_raw = sb("gate_raw", [P, 2])
        gate = sb("gate", [P, 2])
        gate3 = sb("gate3", [P, 1])
        ident = sb("ident", [P, P])
        head_ab = sb("head_ab", [P, 2, HG])
        head_mask = sb("head_mask", [P, HG])
        stats = sb("stats", [P, 2, 6])
        mv = sb("mv", [P, 2, 2, 2])
        var_eps = sb("var_eps", [P, 2])
        var_x = sb("var_x", [P, 1])
        var_b_eps = sb("var_b_eps", [P, 2])
        rstd_b = sb("rstd_b", [P, 2, 2])
        scale_in = sb("scale_in", [P, 2, 2])
        minus_half = sb("minus_half", [P, 2])
        eps = sb("eps", [P, 2])
        norm = sb("norm", [P, 2, 2, D])
        sT = sb("sT", [P, 2, D])
        tT = sb("tT", [P, 2, D])
        k_st = sb("k_st", [P, 2, 2, L])
        k_mask = sb("k_mask", [P, 2, 2, HG, L])
        q_blk = sb("q_blk", [P, 2, 2, P])
        v_mov = sb("v_mov", [P, 2, NHP, 2, VW])
        row_max = sb("row_max", [P, 2, HEADS])
        prob = sb("prob", [P, 2, HEADS, L])
        probT = sb("probT", [P, 2, NHP, P])
        inv_sum = sb("inv_sum", [P, NHP, 2])
        attn = sb("attn", [P, 2, D])
        attnT = sb("attnT", [P, 2, D])
        stats2 = sb("stats2", [P, 6])
        mv2 = sb("mv2", [P, 2, 2])
        xT_f32 = sb("xT_f32", [P, 2, D])
        xn2 = sb("xn2", [P, 2, D])
        order = sb("order", [P, E])
        top1 = sb("top1", [P, NT])
        top2 = sb("top2", [P, NT])
        rank = sb("rank", [P, NT])
        share = sb("share", [P, NT])
        wgt = sb("wgt", [P, NT, E])
        wb = [t[:, 0:CH * E * P].rearrange("p (k e q) -> p k e q", k=CH, e=E)
              for t in (w_raw, c_sb[:, :, :].rearrange("p t d -> p (t d)"))]
        prob_flat = prob[:, :, :, :].rearrange("p b h k -> p (b h k)")
        h = prob_flat[:, 0:FH * CT].rearrange("p (f q) -> p f q", f=FH)
        uw = prob_flat[:, FH * CT:2 * FH * CT].rearrange("p (f q) -> p f q", f=FH)
        yT = k_mask[:, 0, :, :, :].rearrange("p a h k -> p (a h k)")[:, 0:CT]
        h_hi = sb("h_hi", [P, 2, FH, CT], F32R)
        h_lo = sb("h_lo", [P, 2, FH, CT], F32R)

        def routing_place(half, k):
            return c_sb[:, k, :] if half == 0 else probT[:, 0, k, :]

        def by_tile(v):
            return v.rearrange("p (t e) -> p t e", e=E)

        WGT_T = 5

        ps = stack.enter_context(nc.psum_tensor("ps", [P, 8, 512], F32))
        p_in = ps[:, 0, 0:2 * D].rearrange("p (a d) -> p a d", a=2)
        p_x2 = ps[:, 0, 2 * D:3 * D]
        p_x2_late = ps[:, 6, 0:D]
        p_q = ps[:, 1, 0:2 * L].rearrange("p (a l) -> p a l", a=2)
        p_v = ps[:, 1, 256:256 + 2 * CG].rearrange("p (a h d) -> p a h d", a=2, d=HD)
        p_s = ps[:, 2:4, :].rearrange("p g (h k) -> p (g h) k", k=L)
        p_pT = ps[:, 4:6, :]
        p_o = ps[:, 6, 0:NHP * 2 * VW].rearrange("p (h b v) -> p h b v", h=NHP, b=2)
        p_out = ps[:, 7, 0:D]
        p_k = ps[:, 7, D:D + 2 * L].rearrange("p (a l) -> p a l", a=2)
        p_wT = ps[:, 7, D:D + P]
        p_logit = ps[:, 7, 2 * D:2 * D + NT * E].rearrange("p (t e) -> p t e", e=E)

        x_in = [sem(f"x_in{i}") for i in range(4)]
        c_in = [sem(f"c_in{i}") for i in range(4)]
        w_in = sem("w_in")
        small_in = sem("small_in")
        w_all_in = sem("w_all_in")
        out_done = sem("out_done")
        ident_zero = sem("ident_zero")
        consts_ready = sem("consts_ready")
        mask_step = sem("mask_step")
        mask_ready = sem("mask_ready")
        v_static = sem("v_static")
        gate_ready = sem("gate_ready")
        stats_done = sem("stats_done")
        aggr_done = sem("aggr_done")
        scale_step = sem("scale_step")
        scale_ready = sem("scale_ready")
        var2_done = sem("var2_done")
        tail_step = sem("tail_step")
        norm_ready = sem("norm_ready")
        norm_turned = sem("norm_turned")
        sT_ready = sem("sT_ready")
        k_ready = sem("k_ready")
        qv_ready = sem("qv_ready")
        k_out = sem("k_out")
        q_out = sem("q_out")
        v_out = sem("v_out")
        k_masked = sem("k_masked")
        s_ready = sem("s_ready")
        max_done = sem("max_done")
        s_shifted = sem("s_shifted")
        exp_done = sem("exp_done")
        prob_turned = sem("prob_turned")
        probT_done = sem("probT_done")
        o_ready = sem("o_ready")
        inv_done = sem("inv_done")
        attn_ready = sem("attn_ready")
        attn_turned = sem("attn_turned")
        attnT_ready = sem("attnT_ready")
        fc_ready = sem("fc_ready")
        x2_ready = sem("x2_ready")
        stats2_done = sem("stats2_done")
        aggr2_done = sem("aggr2_done")
        xT_f32_ready = sem("xT_f32_ready")
        xn2_ready = sem("xn2_ready")
        xn2_turned = sem("xn2_turned")
        xT_lo_ready = sem("xT_lo_ready")
        w_hi_ready = sem("w_hi_ready")
        w_split = sem("w_split")
        logits_ready = sem("logits_ready")
        gate_exp = sem("gate_exp")
        route = sem("route")
        g_ready = sem("g_ready")
        u_ready = sem("u_ready")
        silu_done = sem("silu_done")
        h_done = sem("h_done")
        h_hi_done = sem("h_hi_done")
        h_lo_done = sem("h_lo_done")
        y_ready = sem("y_ready")
        wgt_ready = sem("wgt_ready")
        wgt_turned = sem("wgt_turned")
        wgtT_ready = sem("wgtT_ready")
        wgt_stored = sem("wgt_stored")
        wb_first = sem("wb_first")
        wb_in = [sem("wb_even_in"), sem("wb_odd_in")]
        uw_done = sem("uw_done")
        yT_ready = sem("yT_ready")
        y_turned = sem("y_turned")
        result_ready = sem("result_ready")

        block = stack.enter_context(nc.Block())

        FIRST, LAST = -3, NT + 5
        LOOP_FROM = 6
        LOOP_TO = LOOP_FROM + 2 * ((NT - 3 - LOOP_FROM) // 2)

        def attention_steps(eng, step, first, unit):
            for t in range(FIRST, LOOP_FROM):
                step(t, t % 2)
            with eng.Fori(0, (LOOP_TO - LOOP_FROM) // 2) as j:
                for u in range(2):
                    step(j * 2 + (LOOP_FROM + u), (LOOP_FROM + u) % 2)
            for t in range(LOOP_TO, LAST + 1):
                step(t, t % 2)
                if t == NT:
                    first()
                if NT < t < LAST:
                    unit(0, t - NT - 1, True)

        def within(i):
            return not isinstance(i, int) or 0 <= i < NT

        def reused(i, n=2):
            return not isinstance(i, int) or i >= n

        UNITS = 2 * NE
        EARLY = LAST - NT - 1

        def expert_units(unit, eng):
            for n in range(EARLY, UNITS):
                unit(0, n, True)
            with eng.Fori(1, NC // 2 - 1) as j:
                for n in range(UNITS):
                    unit(j, n, True)
            for n in range(UNITS):
                unit(NC // 2 - 1, n, n < UNITS - 1)

        def chunk_half(n):
            n = n % UNITS
            return n if n < 2 else (n - 2) // E

        def chunk_of(j, n):
            return (j + n // UNITS) * 2 + chunk_half(n)

        def expert_of(n):
            return E if n % UNITS < 2 else (n - 2) % E

        def chunk_before(j, n, slots):
            if n == E + 2 + slots:
                return j * 2
            if n == slots and not (isinstance(j, int) and j == 0):
                return j * 2 - 1
            return None

        def up_bank(f, which):
            return 2 * (1 - f) + which

        def w_up(w, e, which, f):
            at = e * UP + which * F + f * P
            return w[:, at:at + P]

        def w_down(w, e, f):
            at = WUP + (e * FH + f) * D
            return w[:, at:at + D]

        def xT_tile(t, i):
            flat = t[:, :, :].rearrange("p c t -> p (c t)")
            return flat[:, i * P:(i + 1) * P] if isinstance(i, int) else flat[:, bass.ts(i, P)]

        def splits(t):
            return not isinstance(t, int) or WS_FROM <= t < WS_FROM + SPLITS

        def w_slice(t):
            t = t - WS_FROM
            return slice(t * WSL, (t + 1) * WSL) if isinstance(t, int) else bass.ts(t, WSL)

        ROUTE_PARTS = 5
        EXP_STEP = NT - 4
        ROUTE_STEP = NT - 3
        TURN_STEP = NT + 1
        EXP_SLOT = 4
        ROUTE_SLOT = 5
        TURN_SLOT = 11

        def x2_bank(t):
            return p_x2_late if isinstance(t, int) and t > NT else p_x2

        IN_FROM = [0, 4, LOOP_FROM + 2, 20]

        @block.sync
        def _(sp):
            for k, (i0, i1) in enumerate(zip(IN_FROM, IN_FROM[1:] + [NT])):
                sp.dma_start(c_sb[:, i0:i1, :], ct[:, i0:i1, :]).then_inc(c_in[k], 16)
                sp.dma_start(x_sb[:, i0:i1, :], xt[:, i0:i1, :]).then_inc(x_in[k], 16)
                if k == 0:
                    sp.wait_ge(small_in, 16 * 7)
                    sp.wait_ge(w_in, 64)
            up = w_raw[:, 0:WUP].rearrange("p (e w f) -> p e w f", e=NE, w=2)
            down = w_raw[:, WUP:WALL].rearrange("p (e d) -> p e d", e=NE * FH)
            sp.dma_start(up[:, 0:E, 0, :], we1.rearrange("e d f -> d e f")).then_inc(w_all_in, 16)
            sp.dma_start(up[:, 0:E, 1, :], we3.rearrange("e d f -> d e f")).then_inc(w_all_in, 16)
            sp.dma_start(up[:, E, 0, :], ws1).then_inc(w_all_in, 16)
            sp.dma_start(up[:, E, 1, :], ws3).then_inc(w_all_in, 16)
            sp.dma_start(down[:, 0:E * FH, :], we2.rearrange("e (h f) d -> f (e h) d", f=P)).then_inc(w_all_in, 16)
            sp.dma_start(down[:, E * FH:NE * FH, :], ws2.rearrange("(h f) d -> f h d", f=P)).then_inc(w_all_in, 16)

            def store_weights(half):
                sp.wait_ge(wgtT_ready, half + 1)
                rows = w_dram[half * HT:(half + 1) * HT, :, :].rearrange("t e q -> (t e) q")
                sp.dma_start(rows, routing_place(half, WGT_T)).then_inc(wgt_stored, 16)

            store_weights(0)
            sp.wait_ge(w_split, SPLITS)
            for c in range(NC + 2):
                if c < NC:
                    if c == 2:
                        store_weights(1)
                    if c in (0, NC // 2):
                        sp.wait_ge(wgt_stored, 16 if c == 0 else 32)
                    if c >= 2:
                        units = (c // 2 - 1) * UNITS + (E + 2 if c % 2 == 0 else UNITS)
                        sp.wait_ge(uw_done, FH * units)
                    src = w_dram[c * CH:(c + 1) * CH, :, :]
                    if c == 0:
                        some, rest = src[:, 0:2, :], src[:, 2:E, :]
                        sp.dma_start(wb[0][:, :, 0:2, :], some.partition_broadcast(P)).then_inc(wb_first, 16)
                        sp.dma_start(wb[0][:, :, 2:E, :], rest.partition_broadcast(P)).then_inc(wb_in[0], 16)
                    else:
                        sp.dma_start(wb[c % 2], src.partition_broadcast(P)).then_inc(wb_in[c % 2], 16)
                if c >= 2:
                    o = slice((c - 2) * CH, (c - 1) * CH)
                    sp.wait_ge(result_ready, c - 1)
                    sp.dma_start(ot[:, o, :], x_sb[:, o, :]).then_inc(out_done, 16)
            sp.wait_ge(out_done, 16 * NC)

        @block.gpsimd
        def _(pool):
            pool.memset(ident[:, :], 0.0).then_inc(ident_zero, 1)
            pool.memset(head_ab[:, :, :], 1.0).then_inc(mask_step, 1)
            pool.wait_ge(ident_zero, 1)
            pool.affine_select(out=ident[:, :], in_=ident[:, :], compare_op=ALU.not_equal, fill=1.0, base=0,
                               pattern=[[-1, P]], channel_multiplier=1).then_inc(consts_ready, 1)
            pool.wait_ge(mask_step, 1)
            pool.affine_select(out=head_ab[:, :, :], in_=head_ab[:, :, :], compare_op=ALU.is_ge, fill=0.0, base=0,
                               pattern=[[-CG, 2], [-HD, HG]], channel_multiplier=1).then_inc(mask_step, 1)
            pool.wait_ge(mask_step, 2)
            pool.affine_select(out=head_ab[:, :, :], in_=head_ab[:, :, :], compare_op=ALU.is_ge, fill=0.0,
                               base=HD - 1, pattern=[[CG, 2], [HD, HG]], channel_multiplier=-1).then_inc(mask_step, 1)
            pool.wait_ge(mask_step, 3)
            pool.tensor_tensor(head_mask[:, :], head_ab[:, 0, :], head_ab[:, 1, :], ALU.add).then_inc(mask_ready, 1)
            pool.wait_ge(mask_ready, 1)
            for e in range(E):
                i = pool.memset(order[:, e:e + 1], float(E - e))
            i.then_inc(consts_ready, 1)
            pool.memset(minus_half[:, :], -0.5)
            pool.memset(eps[:, :], EPS).then_inc(scale_step, 1)
            pool.wait_ge(scale_step, 1)
            SC = 6

            def variance_late(i, b):
                pool.wait_ge(aggr2_done, i + 1)
                pool.tensor_tensor(var_b_eps[:, 1:2], mv2[:, b, 1:2], eps[:, 0:1], ALU.add).then_inc(var2_done, 1)
                pool.wait_ge(var2_done, i + 1)

            def scale_late(i, b):
                pool.wait_ge(xn2_ready, i - 1)
                pool.tensor_tensor(rstd_b[:, b, 1:2], var_b_eps[:, 1:2], minus_half[:, 1:2],
                                   ALU.pow).then_inc(tail_step, 1)
                pool.wait_ge(tail_step, i - (NT - 6) + 1)

            def step(t, b):
                m = 1 - b
                i = t + 2
                i2 = t - 4
                if within(i):
                    pool.wait_ge(aggr_done, i + 1)
                    if reused(i):
                        pool.wait_ge(norm_ready, i - 1)
                    at = i * SC + 1
                    one = scale_in[:, b, 1:2]
                    pool.tensor_tensor(var_eps[:, :], mv[:, b, :, 1], eps[:, :], ALU.add).then_inc(scale_step, 1)
                    pool.wait_ge(scale_step, at + 1)
                    pool.tensor_tensor(scale_in[:, b, :], var_eps[:, :], minus_half[:, :],
                                       ALU.pow).then_inc(scale_step, 1)
                    pool.wait_ge(scale_step, at + 2)
                    pool.tensor_tensor(var_x[:, :], mv[:, b, 1, 1:2], one, ALU.mult).then_inc(scale_step, 1)
                    pool.wait_ge(scale_step, at + 3)
                    pool.tensor_tensor(var_x[:, :], var_x[:, :], one, ALU.mult).then_inc(scale_step, 1)
                    pool.wait_ge(scale_step, at + 4)
                    pool.tensor_tensor(var_b_eps[:, 0:1], var_x[:, :], eps[:, 0:1], ALU.add).then_inc(scale_step, 1)
                if within(i2) and not (isinstance(t, int) and t > NT):
                    variance_late(i2, b)
                if within(i):
                    pool.wait_ge(scale_step, at + 5)
                    cols = slice(0, 2 if within(i2) else 1)
                    if within(i2) and reused(i2):
                        pool.wait_ge(xn2_ready, i2 - 1)
                    pool.tensor_tensor(rstd_b[:, b, cols], var_b_eps[:, cols], minus_half[:, cols],
                                       ALU.pow).then_inc(scale_step, 1)
                    pool.wait_ge(scale_step, at + 6)
                    pool.tensor_tensor(one, rstd_b[:, b, 0:1], one, ALU.mult).then_inc(scale_ready, 1)
                    pool.wait_ge(scale_ready, i + 1)
                elif within(i2) and t <= NT:
                    scale_late(i2, b)
                i = t + 1
                if within(i):
                    pool.wait_ge(k_out, i + 1)
                    if reused(i):
                        pool.wait_ge(s_ready, i - 1)
                    shape = [P, 2, HG, L]
                    pool.tensor_tensor(k_mask[:, m, :, :, :],
                                       k_st[:, m, :, :].unsqueeze(2).broadcast_to(shape),
                                       head_mask[:, :].unsqueeze(1).unsqueeze(3).broadcast_to(shape),
                                       ALU.mult).then_inc(k_masked, 1)
                i = t - 5
                if within(i):
                    pool.wait_ge(xT_f32_ready, i + 1)
                    pool.tensor_tensor(xT_tile(xT_lo, i), xT_f32[:, m, :], xT_tile(xT_hi, i).bitcast(F32),
                                       ALU.subtract).then_inc(xT_lo_ready, 1)
                if splits(t):
                    pool.wait_ge(w_hi_ready, t - WS_FROM + 1)
                    s = w_slice(t)
                    pool.tensor_tensor(w_lo[:, s], w_raw[:, s], w_hi[:, s].bitcast(F32),
                                       ALU.subtract).then_inc(w_split, 1)
                i = t - 3
                if isinstance(t, int) and t >= NT and within(i):
                    variance_late(i, m)
                    scale_late(i, m)

            def low(j, n):
                u = j * UNITS + n
                m = n % 2
                for f in range(FH):
                    pool.wait_ge(h_hi_done, u * FH + f + 1)
                    pool.tensor_tensor(h_lo[:, m, f, :], h[:, f, :], h_hi[:, m, f, :].bitcast(F32),
                                       ALU.subtract).then_inc(h_lo_done, 1)

            def unit(j, n, more):
                if more:
                    low(j, n + 1)

            attention_steps(pool, step, lambda: low(0, 0), unit)
            expert_units(unit, pool)

        @block.scalar
        def _(act):
            for t, src in ((wq_sb, wq), (wk_sb, wk), (wv_sb, wv), (wfc_sb, wfc)):
                act.dma_start(t[:, :], src).then_inc(w_in, 16)
            for k, src in enumerate((ln1_g, ln1_b, ln2_g, ln2_b)):
                act.dma_start(ln_sb[:, k:k + 1], src.rearrange("(d a) -> d a", a=1)).then_inc(small_in, 16)
            for k, src in enumerate((g_xattn, g_ffn)):
                act.dma_start(gate_raw[:, k:k + 1], src.partition_broadcast(P)).then_inc(small_in, 16)
            act.dma_start(wg_raw[:, :], wg).then_inc(small_in, 16)
            act.wait_ge(small_in, 16 * 7)
            act.activation(gate[:, :], gate_raw[:, :], ACT.Tanh).then_inc(gate_ready, 1)

            def gate_exponentials(half):
                act.activation(by_tile(routing_place(half, 0)), p_logit[:, half * HT:(half + 1) * HT, :], ACT.Exp,
                               scale=-1.0).then_inc(gate_exp, 1)

            def take_weights(half):
                act.wait_ge(wgt_turned, half + 1)
                act.activation(routing_place(half, WGT_T), p_wT, ACT.Copy).then_inc(wgtT_ready, 1)

            def step(t, b):
                m = 1 - b
                i = t - 1
                if within(i):
                    act.wait_ge(s_shifted, i + 1)
                    act.activation(prob[:, m, :, :], prob[:, m, :, :], ACT.Exp, scale=SCALE).then_inc(exp_done, 1)
                if within(t):
                    if isinstance(t, int) and t == 0:
                        act.wait_ge(v_static, 2)
                    if reused(t):
                        act.wait_ge(o_ready, t - 1)
                    for s in range(2):
                        r = slice(L * s, L * s + L)
                        last = act.activation(v_mov[r, b, :, :, HD * s:HD * s + HD],
                                              p_v[r, :, :, :].rearrange("p a h d -> p h a d"), ACT.Copy)
                    last.then_inc(v_out, 1)
                i = t + 1
                if within(i):
                    act.wait_ge(norm_turned, i + 1)
                    if reused(i):
                        act.wait_ge(qv_ready, i - 1)
                    act.activation(sT[:, m, :], p_in[:, 0, :], ACT.Identity, bias=ln_sb[:, 1:2], scale=ln_sb[:, 0:1])
                    act.activation(tT[:, m, :], p_in[:, 1, :], ACT.Identity, bias=ln_sb[:, 3:4],
                                   scale=ln_sb[:, 2:3]).then_inc(sT_ready, 1)
                if within(t + 1):
                    act.wait_ge(k_ready, t + 2)
                if within(t - 2):
                    act.wait_ge(attn_turned, t - 1)
                if isinstance(t, int) and t == EXP_STEP:
                    gate_exponentials(0)
                if isinstance(t, int) and t == TURN_STEP:
                    take_weights(0)
                i = t + 1
                if within(i):
                    if reused(i):
                        act.wait_ge(k_masked, i - 1)
                    act.activation(k_st[:, m, :, :], p_k, ACT.Copy).then_inc(k_out, 1)
                i = t - 2
                if within(i):
                    if reused(i):
                        act.wait_ge(fc_ready, i - 1)
                    act.activation(attnT[:, b, :], p_out, ACT.Copy).then_inc(attnT_ready, 1)
                i = t - 1
                if within(i):
                    for half in range(2):
                        act.wait_ge(prob_turned, i * 2 + half + 1)
                        if reused(i) and half == 0:
                            act.wait_ge(o_ready, i - 1)
                        pairs = slice(half * NHP // 2, (half + 1) * NHP // 2)
                        act.activation(probT[:, m, pairs, :].rearrange("p h q -> p (h q)"), p_pT[:, half, :],
                                       ACT.Copy).then_inc(probT_done, 1)
                i = t + 1
                if within(i):
                    act.wait_ge(qv_ready, i + 1)
                    if reused(i):
                        act.wait_ge(s_ready, i - 1)
                    if isinstance(i, int) and i == 0:
                        act.wait_ge(v_static, 1)
                    for s in range(2):
                        r = slice(L * s, L * s + L)
                        last = act.activation(q_blk[r, m, :, r], p_q[r, :, :], ACT.Copy)
                    last.then_inc(q_out, 1)
                i = t - 5
                if within(i):
                    act.wait_ge(xn2_turned, i + 1)
                    act.activation(xT_tile(xT_hi, i), x2_bank(t), ACT.Copy)
                    if reused(i):
                        act.wait_ge(xT_lo_ready, i - 1)
                        act.wait_ge(logits_ready, i - 1)
                    act.activation(xT_f32[:, m, :], x2_bank(t), ACT.Copy).then_inc(xT_f32_ready, 1)
                if splits(t):
                    if isinstance(t, int) and t == WS_FROM:
                        act.wait_ge(w_all_in, 96)
                    s = w_slice(t)
                    act.activation(w_hi[:, s], w_raw[:, s], ACT.Copy).then_inc(w_hi_ready, 1)

            def silu(j, n):
                u = j * UNITS + n
                for f in range(FH):
                    act.wait_ge(g_ready, u * FH + f + 1)
                    act.activation(ps[:, up_bank(f, 0), :], ps[:, up_bank(f, 0), :], ACT.Silu).then_inc(silu_done, 1)

            def high(j, n):
                u = j * UNITS + n
                m = n % 2
                for f in range(FH):
                    act.wait_ge(h_done, u * FH + f + 1)
                    if not (isinstance(j, int) and j == 0 and n < 2):
                        act.wait_ge(y_ready, u - 1)
                    act.activation(h_hi[:, m, f, :], h[:, f, :], ACT.Copy).then_inc(h_hi_done, 1)


            def unit(j, n, more):
                if isinstance(j, int) and (j, n) == (0, 0):
                    high(0, 0)
                if more:
                    silu(j, n + 1)
                    high(j, n + 1)
                if isinstance(j, int) and (j, n) == (0, EXP_SLOT):
                    act.wait_ge(logits_ready, NT)
                    gate_exponentials(1)
                if isinstance(j, int) and (j, n) == (0, TURN_SLOT):
                    take_weights(1)
                c = chunk_before(j, n, 0)
                if c is not None:
                    take_sums(c, chunk_half(n - 1) if n else 1, j * UNITS + n)

            def take_sums(c, m, units):
                act.wait_ge(y_ready, units)
                if not (isinstance(c, int) and c == 0):
                    act.wait_ge(y_turned, c)
                act.activation(yT, ps[:, 4 + m, :], ACT.Copy).then_inc(yT_ready, 1)

            attention_steps(act, step, lambda: silu(0, 0), unit)
            expert_units(unit, act)
            take_sums(NC - 1, 1, NC * NE)

        @block.vector
        def _(dve):
            dve.memset(q_blk[:, :, :, :], 0.0)
            dve.memset(v_mov[:, :, :, :, :], 0.0).then_inc(v_static, 1)
            dve.wait_ge(v_static, 1)
            dve.memset(v_mov[0:L, :, :, :, 2 * HD:2 * HD + 1], 1.0)
            dve.memset(v_mov[L:P, :, :, :, 2 * HD + 1:2 * HD + 2], 1.0).then_inc(v_static, 1)

            count = [0]

            def then(instruction):
                count[0] += 1
                instruction.then_inc(route, 1)
                dve.wait_ge(route, count[0])

            full = [P, HT, E]

            def spread(v):
                return v.unsqueeze(2).broadcast_to(full)

            def routing(half, part):
                tiles = slice(half * HT, (half + 1) * HT)
                gt, gt2, pick1, pick2, key = (by_tile(routing_place(half, k)) for k in range(5))
                late = order[:, :].unsqueeze(1).broadcast_to(full)

                def pick(scores, top, picked):
                    then(dve.tensor_tensor(key, scores, spread(top), ALU.is_equal))
                    then(dve.tensor_tensor(key, key, late, ALU.mult))
                    then(dve.tensor_reduce(rank[:, tiles], key, AX_X, ALU.max))
                    then(dve.tensor_tensor(picked, key, spread(rank[:, tiles]), ALU.is_equal))

                if part == 0:
                    if half == 0:
                        then(dve.tensor_scalar(gate3[:, :], gate[:, 1:2], 1.0 / 3.0, None, ALU.mult))
                    dve.wait_ge(gate_exp, half + 1)
                    then(dve.tensor_scalar(gt, gt, 1.0, None, ALU.add))
                    then(dve.reciprocal(gt, gt))
                    then(dve.tensor_reduce(top1[:, tiles], gt, AX_X, ALU.max))
                if part == 1:
                    dve.wait_ge(consts_ready, 2)
                    pick(gt, top1[:, tiles], pick1)
                if part == 2:
                    then(dve.scalar_tensor_tensor(out=gt2, in0=pick1, scalar=-4.0, in1=gt, op0=ALU.mult, op1=ALU.add))
                    then(dve.tensor_reduce(top2[:, tiles], gt2, AX_X, ALU.max))
                    then(dve.tensor_tensor(share[:, tiles], top1[:, tiles], top2[:, tiles], ALU.add))
                    then(dve.reciprocal(share[:, tiles], share[:, tiles]))
                if part == 3:
                    pick(gt2, top2[:, tiles], pick2)
                if part == 4:
                    then(dve.tensor_scalar(share[:, tiles], share[:, tiles], gate3[:, 0:1], None, ALU.mult))
                    then(dve.tensor_tensor(top1[:, tiles], top1[:, tiles], share[:, tiles], ALU.mult))
                    then(dve.tensor_tensor(top2[:, tiles], top2[:, tiles], share[:, tiles], ALU.mult))
                    then(dve.tensor_tensor(pick1, pick1, spread(top1[:, tiles]), ALU.mult))
                    then(dve.tensor_tensor(pick2, pick2, spread(top2[:, tiles]), ALU.mult))
                    dve.tensor_tensor(wgt[:, tiles, :], pick1, pick2, ALU.add).then_inc(wgt_ready, 1)

            def normalise(i, b):
                if within(i):
                    dve.wait_ge(scale_ready, i + 1)
                    if reused(i):
                        dve.wait_ge(norm_turned, i - 1)
                    dve.tensor_scalar(norm[:, b, 0, :], c_sb[:, i, :], mv[:, b, 0, 0:1], scale_in[:, b, 0:1],
                                      ALU.subtract, ALU.mult)
                    dve.tensor_scalar(norm[:, b, 1, :], x_sb[:, i, :], mv[:, b, 1, 0:1], scale_in[:, b, 1:2],
                                      ALU.subtract, ALU.mult).then_inc(norm_ready, 1)

            def step(t, b):
                m = 1 - b
                if isinstance(t, int) and 0 <= t - ROUTE_STEP < ROUTE_PARTS - 1:
                    routing(0, t - ROUTE_STEP)
                if isinstance(t, int) and t - ROUTE_STEP == ROUTE_PARTS - 2:
                    routing(0, ROUTE_PARTS - 1)
                if within(t + 3):
                    if reused(t + 3, 1):
                        dve.wait_ge(aggr_done, t + 3)
                    if reused(t + 3):
                        dve.wait_ge(norm_ready, t + 2)
                i = t - 3
                norm_first = isinstance(t, int) and t < 1
                if norm_first:
                    normalise(t + 2, b)
                if within(t):
                    dve.wait_ge(s_ready, t + 1)
                    if reused(t):
                        dve.wait_ge(prob_turned, (t - 1) * 2)
                    dve.tensor_reduce(row_max[:, b, :], p_s, AX_X, ALU.max).then_inc(max_done, 1)
                    dve.wait_ge(max_done, t + 1)
                    if within(i):
                        dve.wait_ge(x2_ready, i + 1)
                        if reused(i, 1):
                            dve.wait_ge(aggr2_done, i)
                    dve.tensor_tensor(prob[:, b, :, :], p_s,
                                      row_max[:, b, :].unsqueeze(2).broadcast_to([P, HEADS, L]),
                                      ALU.subtract).then_inc(s_shifted, 1)
                elif within(i):
                    dve.wait_ge(x2_ready, i + 1)
                    dve.wait_ge(aggr2_done, i)
                if within(i):
                    dve.bn_stats(stats2[:, :], x_sb[:, i, :]).then_inc(stats2_done, 1)
                i = t + 3
                if within(i):
                    for k in range(4):
                        if isinstance(i, int) and i == min(IN_FROM[k], LOOP_FROM + 2):
                            dve.wait_ge(c_in[k], 16)
                            dve.wait_ge(x_in[k], 16)
                    dve.bn_stats(stats[:, 0, :], c_sb[:, i, :])
                    dve.bn_stats(stats[:, 1, :], x_sb[:, i, :]).then_inc(stats_done, 1)
                if not norm_first:
                    normalise(t + 2, b)
                i = t - 4
                if within(i):
                    if within(t + 2):
                        dve.wait_ge(scale_ready, t + 3)
                    else:
                        dve.wait_ge(tail_step, i - (NT - 6) + 1)
                    if reused(i):
                        dve.wait_ge(xn2_turned, i - 1)
                    dve.tensor_scalar(xn2[:, b, :], x_sb[:, i, :], mv2[:, b, 0:1], rstd_b[:, b, 1:2], ALU.subtract,
                                      ALU.mult).then_inc(xn2_ready, 1)
                i = t - 2
                if within(i):
                    dve.wait_ge(fc_ready, i + 1)
                    if isinstance(i, int) and i == 0:
                        dve.wait_ge(gate_ready, 1)
                    dve.scalar_tensor_tensor(out=x_sb[:, i, :], in0=p_out, scalar=gate[:, 0:1], in1=x_sb[:, i, :],
                                             op0=ALU.mult, op1=ALU.add).then_inc(x2_ready, 1)
                if within(t - 3):
                    dve.wait_ge(stats2_done, t - 2)
                    if reused(t - 3):
                        dve.wait_ge(xn2_ready, t - 4)
                if within(t + 3):
                    dve.wait_ge(stats_done, t + 4)
                i = t - 1
                if within(i):
                    dve.wait_ge(o_ready, i + 1)
                    for s in range(2):
                        r = slice(L * s, L * s + L)
                        last = dve.reciprocal(inv_sum[r, :, :], p_o[r, :, s, 2 * HD:VW])
                    last.then_inc(inv_done, 1)
                if within(t - 3):
                    dve.bn_aggr(mv2[:, m, :], stats2[:, :]).then_inc(aggr2_done, 1)
                if within(t + 3):
                    dve.bn_aggr(mv[:, m, 0, :], stats[:, 0, :])
                    dve.bn_aggr(mv[:, m, 1, :], stats[:, 1, :]).then_inc(aggr_done, 1)
                if within(i):
                    dve.wait_ge(inv_done, i + 1)
                    if reused(i):
                        dve.wait_ge(attn_turned, i - 1)
                    for s in range(2):
                        r = slice(L * s, L * s + L)
                        last = dve.tensor_tensor(
                            attn[r, m, :].rearrange("p (h s d) -> p h s d", s=2, d=HD),
                            p_o[r, :, s, 0:2 * HD].rearrange("p h (s d) -> p h s d", s=2),
                            inv_sum[r, :, :].unsqueeze(3).broadcast_to([L, NHP, 2, HD]), ALU.mult)
                    last.then_inc(attn_ready, 1)
            def hidden(j, n):
                u = j * UNITS + n
                e = expert_of(n)
                m = chunk_half(n)
                first = isinstance(j, int) and j == 0
                for f in range(FH):
                    dve.wait_ge(u_ready, u * FH + f + 1)
                    if e == 0 and f == 0:
                        if first and not m:
                            dve.wait_ge(wb_first, 16)
                        elif not m:
                            dve.wait_ge(wb_in[0], (j + 1) * 16)
                        else:
                            dve.wait_ge(wb_in[1], (j + 1) * 16)
                    if e == 2 and f == 0 and first and not m:
                        dve.wait_ge(wb_in[0], 16)
                    if not (first and n == 0):
                        dve.wait_ge(h_done, (u - 1) * FH + f + 1)
                    if e == E:
                        dve.tensor_scalar(uw[:, f, :], ps[:, up_bank(f, 1), :], gate3[:, 0:1], None,
                                          ALU.mult).then_inc(uw_done, 1)
                    else:
                        dve.tensor_tensor(uw[:, f, :].rearrange("p (k q) -> p k q", k=CH),
                                          ps[:, up_bank(f, 1), :].rearrange("p (k q) -> p k q", k=CH),
                                          wb[m][:, :, e, :], ALU.mult).then_inc(uw_done, 1)
                for f in range(FH):
                    dve.wait_ge(silu_done, u * FH + f + 1)
                    dve.wait_ge(uw_done, u * FH + f + 1)
                    if not (first and n == 0):
                        dve.wait_ge(h_lo_done, (u - 1) * FH + f + 1)
                    dve.tensor_tensor(h[:, f, :], ps[:, up_bank(f, 0), :], uw[:, f, :], ALU.mult).then_inc(h_done, 1)

            def add_sums(c):
                o = slice(c * CH, (c + 1) * CH) if isinstance(c, int) else bass.ts(c, CH)
                dve.wait_ge(y_turned, c + 1)
                dve.tensor_tensor(x_sb[:, o, :], ps[:, 6, :].rearrange("p (k d) -> p k d", k=CH), x_sb[:, o, :],
                                  ALU.add).then_inc(result_ready, 1)

            def unit(j, n, more):
                if more:
                    hidden(j, n + 1)
                if isinstance(j, int) and j == 0 and 0 <= n - ROUTE_SLOT < ROUTE_PARTS:
                    routing(1, n - ROUTE_SLOT)
                c = chunk_before(j, n, 1)
                if c is not None:
                    add_sums(c)

            attention_steps(dve, step, lambda: hidden(0, 0), unit)
            expert_units(unit, dve)
            add_sums(NC - 1)

        @block.tensor
        def _(pe):
            pe.wait_ge(consts_ready, 1)
            pe.wait_ge(w_in, 64)

            def turn_weights(half):
                pe.wait_ge(wgt_ready, half + 1)
                flat = wgt[:, half * HT:(half + 1) * HT, :].rearrange("p t e -> p (t e)")
                pe.transpose(p_wT, flat, ident[:, :]).then_inc(wgt_turned, 1)

            def step(t, b):
                m = 1 - b
                if isinstance(t, int) and t == NT:
                    pe.wait_ge(w_split, SPLITS)
                    pe.wait_ge(xT_lo_ready, 2 * CH)
                    pe.wait_ge(s_shifted, NT)
                    up_half(0, 0, 0)
                i = t + 1
                if within(i):
                    pe.wait_ge(norm_ready, i + 1)
                    if reused(i, 1):
                        pe.wait_ge(sT_ready, i)
                    if within(t - 6):
                        pe.wait_ge(xT_f32_ready, t - 5)
                    pe.transpose(p_in[:, 0, :], norm[:, m, 0, :], ident[:, :])
                    pe.transpose(p_in[:, 1, :], norm[:, m, 1, :], ident[:, :]).then_inc(norm_turned, 1)
                if within(t):
                    pe.wait_ge(q_out, t + 1)
                    pe.wait_ge(k_masked, t + 1)
                    if reused(t, 1):
                        pe.wait_ge(s_shifted, t)
                    for g in range(2):
                        last = pe.matmul(ps[:, 2 + g, :], q_blk[:, b, g, :],
                                         k_mask[:, b, g, :, :].rearrange("p h k -> p (h k)"), start=True, stop=True)
                    last.then_inc(s_ready, 1)
                if within(t - 3) or within(t - 6):
                    pe.wait_ge(x2_ready, min(t - 2, NT) if isinstance(t, int) else t - 2)
                i = t - 6
                if within(i):
                    pe.wait_ge(xT_f32_ready, i + 1)
                    pe.matmul(p_logit[:, i, :], xT_f32[:, b, :], wg_raw[:, :], start=True,
                              stop=True).then_inc(logits_ready, 1)
                i = t + 1
                if within(i):
                    pe.wait_ge(sT_ready, i + 1)
                    if reused(i, 1):
                        pe.wait_ge(k_out, i)
                    for g in range(2):
                        for s in range(2):
                            last = pe.matmul(p_k[L * s:L * s + L, g, :], wk_sb[:, g * CG:(g + 1) * CG],
                                             sT[:, m, L * s:L * s + L], start=True, stop=True)
                    last.then_inc(k_ready, 1)
                if isinstance(t, int) and t == TURN_STEP:
                    turn_weights(0)
                i = t - 2
                if within(i):
                    pe.wait_ge(attn_ready, i + 1)
                    pe.transpose(p_out, attn[:, b, :], ident[:, :]).then_inc(attn_turned, 1)
                i = t - 1
                if within(i):
                    pe.wait_ge(exp_done, i + 1)
                    flat = prob[:, m, :, :].rearrange("p h k -> p (h k)")
                    for half in range(2):
                        if reused(i, 1):
                            pe.wait_ge(probT_done, i * 2 - 1 + half)
                        for hp in range(half * NHP // 2, (half + 1) * NHP // 2):
                            last = pe.transpose(ps[:, 4 + half, (hp % 4) * P:(hp % 4 + 1) * P],
                                                flat[:, hp * P:(hp + 1) * P], ident[:, :])
                        last.then_inc(prob_turned, 1)
                i = t + 1
                if within(i):
                    if reused(i, 1):
                        pe.wait_ge(v_out, i)
                    for g in range(2):
                        for s in range(2):
                            pe.matmul(p_q[L * s:L * s + L, g, :], wq_sb[:, g * CG:(g + 1) * CG],
                                      tT[:, m, L * s:L * s + L], start=True, stop=True)
                    for s in range(2):
                        for o in range(2):
                            last = pe.matmul(p_v[L * o:L * o + L, s, :, :], sT[:, m, L * s:L * s + L],
                                             wv_sb[:, :].rearrange("p (h o d) -> p o h d", o=2, d=HD)[:, o, :, :],
                                             start=True, stop=True)
                    last.then_inc(qv_ready, 1)
                i = t - 2
                if within(i):
                    pe.wait_ge(attnT_ready, i + 1)
                    if within(t + 1):
                        pe.wait_ge(k_out, t + 2)
                    pe.matmul(p_out, attnT[:, b, :], wfc_sb[:, :], start=True, stop=True).then_inc(fc_ready, 1)
                i = t - 5
                if within(i):
                    pe.wait_ge(xn2_ready, i + 1)
                    if not within(t + 1) and reused(i, 1):
                        pe.wait_ge(xT_f32_ready, i)
                    if isinstance(t, int) and t == NT + 1:
                        pe.wait_ge(attn_ready, NT)
                    pe.transpose(x2_bank(t), xn2[:, m, :], ident[:, :]).then_inc(xn2_turned, 1)
                i = t - 1
                if within(i):
                    pe.wait_ge(v_out, i + 1)
                    pe.wait_ge(probT_done, i * 2 + 2)
                    if reused(i, 1):
                        pe.wait_ge(attn_ready, i)
                    for hp in range(NHP):
                        last = pe.matmul(p_o[:, hp, :, :].rearrange("p b v -> p (b v)"), probT[:, m, hp, :],
                                         v_mov[:, m, hp, :, :].rearrange("p b v -> p (b v)"), start=True, stop=True)
                    last.then_inc(o_ready, 1)

            def up_half(j, n, f):
                u = j * UNITS + n
                c = chunk_of(j, n)
                e = expert_of(n)
                for which, done, free in ((1, u_ready, uw_done), (0, g_ready, h_done)):
                    if not (isinstance(j, int) and (j, n) == (0, 0)):
                        pe.wait_ge(free, (u - 1) * FH + f + 1)
                    o = ps[:, up_bank(f, which), :]
                    pe.matmul(o, w_up(w_hi, e, which, f), xT_hi[:, c, :], start=True, stop=False)
                    pe.matmul(o, w_up(w_hi, e, which, f), xT_lo[:, c, :], start=False, stop=False)
                    pe.matmul(o, w_up(w_lo, e, which, f), xT_hi[:, c, :], start=False, stop=True).then_inc(done, 1)

            def up(j, n):
                for f in range(FH):
                    up_half(j, n, f)

            def down(j, n):
                u = j * UNITS + n
                e = expert_of(n)
                m = n % 2
                first = isinstance(j, int) and j == 0
                for f in range(FH):
                    pe.wait_ge(h_lo_done, u * FH + f + 1)
                    if f == 0 and e == E and not first:
                        pe.wait_ge(yT_ready, chunk_of(j, n) - 1)
                    o = ps[:, 4 + chunk_half(n), :]
                    head = e == E and f == 0
                    tail = e == E - 1 and f == FH - 1
                    hi = h_hi[:, m, f, :]
                    pe.matmul(o, w_down(w_hi, e, f), hi, start=head, stop=False)
                    pe.matmul(o, w_down(w_lo, e, f), hi, start=False, stop=False)
                    last = pe.matmul(o, w_down(w_hi, e, f), h_lo[:, m, f, :], start=False, stop=tail)
                last.then_inc(y_ready, 1)

            def first():
                pe.wait_ge(xT_f32_ready, NT - 4)
                up_half(0, 0, 1)

            def unit(j, n, more):
                if more:
                    up(j, n + 1)
                down(j, n)
                if isinstance(j, int) and (j, n) == (0, TURN_SLOT):
                    pe.wait_ge(gate_exp, 2)
                    turn_weights(1)
                c = chunk_before(j, n, 1)
                if c is not None:
                    turn_sums(c)

            def turn_sums(c):
                pe.wait_ge(yT_ready, c + 1)
                if not (isinstance(c, int) and c == 0):
                    pe.wait_ge(result_ready, c)
                for k in range(CH):
                    last = pe.transpose(ps[:, 6, k * P:(k + 1) * P], yT[:, k * P:(k + 1) * P], ident[:, :])
                last.then_inc(y_turned, 1)

            attention_steps(pe, step, first, unit)
            pe.wait_ge(xT_lo_ready, NT)
            expert_units(unit, pe)
            turn_sums(NC - 1)


_INS = ['x', 'ctx_1024', 'g_xattn', 'g_ffn', 'L0_xattn_ln1_g', 'L0_xattn_ln1_b', 'L0_xattn_ln2_g', 'L0_xattn_ln2_b',
        'L0_xattn_Wq', 'L0_xattn_Wk', 'L0_xattn_Wv', 'L0_xattn_Wfc', 'L0_ffn_Wg', 'L0_ffn_Ws1', 'L0_ffn_Ws3',
        'L0_ffn_Ws2', 'L0_ffn_We1', 'L0_ffn_We3', 'L0_ffn_We2']
_OUTS = [((64, 64, 128), 'float32')]


def kernel(**inputs):
    import numpy as _np
    import concourse.bacc as _bacc
    from concourse import mybir as _mybir
    from concourse.bass_utils import run_bass_kernel_spmd as _run

    nc = _bacc.Bacc("TRN2", target_bir_lowering=False, num_devices=1)
    arrays, args = {}, []
    for name in _INS:
        a = _np.ascontiguousarray(inputs[name])
        arrays[f"in_{name}_dram"] = a
        args.append(nc.dram_tensor(f"in_{name}_dram", a.shape, _mybir.dt.from_np(a.dtype), kind="ExternalInput").ap())
    for i, (shape, dtype) in enumerate(_OUTS):
        dt = _mybir.dt.from_np(_np.dtype(dtype))
        args.append(nc.dram_tensor(f"out_{i}_dram", shape, dt, kind="ExternalOutput").ap())
    args.append(nc.dram_tensor("routing_weights", (32, 8, 128), _mybir.dt.float32).ap())
    gated_attention_and_experts(nc, *args)
    r = _run(nc, [arrays], core_ids=[0])
    got = tuple(r.results[0][f"out_{i}_dram"] for i in range(len(_OUTS)))
    return got[0]
```
